# Optimizing a Trainium2 kernel written in Bass

```python
import numpy as np
import jax
import jax.numpy as jnp

def _softmax(x, axis=-1):
    return jax.nn.softmax(x, axis=axis)

def _gelu(x):
    return jax.nn.gelu(x, approximate=True)

def _silu(x):
    return jax.nn.silu(x)

def _sigmoid(x):
    return jax.nn.sigmoid(x)

def _layernorm(x, axis=-1, eps=1e-05):
    m = jnp.mean(x, axis=axis, keepdims=True)
    v = jnp.var(x, axis=axis, keepdims=True)
    return (x - m) / jnp.sqrt(v + eps)

def _scatter_add(tgt, idx, src, axis=0):
    return tgt.at[idx].add(src)

def _segment_sum(src, seg, n):
    return jax.ops.segment_sum(src, seg, n)
kernel_name = 'mk_sandwich_d1_jaxref_r8_30a805'

def setup_inputs(seed: int=0):
    np.random.seed(seed)
    _w = jnp.asarray

    def _L0_attn_setup():
        import jax, jax.numpy as jnp
        import numpy as np
        import math
        D_MODEL = 256
        N_HEADS = 16
        D_HEAD = D_MODEL // N_HEADS
        key = jax.random.key(seed)
        ks = jax.random.split(key, 6)
        B, S, D = (4, 256, D_MODEL)
        scale = 1.0 / math.sqrt(D)
        x = jax.random.normal(ks[0], (B, S, D), dtype=jnp.float32)
        Wq = jax.random.normal(ks[1], (D, D), dtype=jnp.float32) * scale
        Wk = jax.random.normal(ks[2], (D, D), dtype=jnp.float32) * scale
        Wv = jax.random.normal(ks[3], (D, D), dtype=jnp.float32) * scale
        Wo = jax.random.normal(ks[4], (D, D), dtype=jnp.float32) * scale
        bo = jax.random.normal(ks[5], (D,), dtype=jnp.float32) * 0.01
        return {'x': x, 'Wq': Wq, 'Wk': Wk, 'Wv': Wv, 'Wo': Wo, 'bo': bo}
    _L0_attn_in = _L0_attn_setup()

    def _L0_ffn_setup():
        import jax, jax.numpy as jnp
        import numpy as np
        B, S, D, H = (4, 256, 256, 1024)

        def fwht(x):
            orig_shape = x.shape
            n = orig_shape[-1]
            x = x.reshape(-1, n)
            h = 1
            while h < n:
                xb = x.reshape(-1, n // (2 * h), 2, h)
                a = xb[:, :, 0, :]
                b = xb[:, :, 1, :]
                x = jnp.stack([a + b, a - b], axis=2).reshape(-1, n)
                h *= 2
            scale = jnp.asarray(1.0 / np.sqrt(n), dtype=x.dtype)
            return (x * scale).reshape(orig_shape)
        key = jax.random.key(seed)
        kx, k1, k2, k3 = jax.random.split(key, 4)
        x = jax.random.normal(kx, (B, S, D), dtype=jnp.float32)
        W1 = jax.random.normal(k1, (H, D), dtype=jnp.float32) * (1.0 / np.sqrt(D))
        W2 = jax.random.normal(k2, (D, H), dtype=jnp.float32) * (1.0 / np.sqrt(H))
        W3 = jax.random.normal(k3, (H, D), dtype=jnp.float32) * (1.0 / np.sqrt(D))
        return {'x': x, 'W1': W1, 'W2': W2, 'W3': W3}
    _L0_ffn_in = _L0_ffn_setup()
    _d = {'L0_attn_x': _L0_attn_in['x'], 'L0_attn_Wq': _L0_attn_in['Wq'], 'L0_attn_Wk': _L0_attn_in['Wk'], 'L0_attn_Wv': _L0_attn_in['Wv'], 'L0_attn_Wo': _L0_attn_in['Wo'], 'L0_attn_bo': _L0_attn_in['bo'], 'L0_ffn_W1': _L0_ffn_in['W1'], 'L0_ffn_W2': _L0_ffn_in['W2'], 'L0_ffn_W3': _L0_ffn_in['W3']}
    _x0 = _d['L0_attn_x']
    _d['L0_attn_x'] = jax.random.normal(jax.random.fold_in(jax.random.key(seed), 1), (4, 1024, 256), dtype=_x0.dtype)
    del _x0
    return _d

def reference(L0_attn_x, L0_attn_Wq, L0_attn_Wk, L0_attn_Wv, L0_attn_Wo, L0_attn_bo, L0_ffn_W1, L0_ffn_W2, L0_ffn_W3):

    def _L0_attn_ref(x, Wq, Wk, Wv, Wo, bo):
        import jax, jax.numpy as jnp
        import numpy as np
        import math
        D_MODEL = 256
        N_HEADS = 16
        D_HEAD = D_MODEL // N_HEADS
        B, S, D = x.shape
        H, Dh = (N_HEADS, D_HEAD)
        q = (x @ Wq.T).reshape(B, S, H, Dh).transpose(0, 2, 1, 3)
        k = (x @ Wk.T).reshape(B, S, H, Dh).transpose(0, 2, 1, 3)
        v = (x @ Wv.T).reshape(B, S, H, Dh).transpose(0, 2, 1, 3)
        scores = jnp.einsum('bhqd,bhkd->bhqk', q, k) / math.sqrt(Dh)
        causal = jnp.tril(jnp.ones((S, S), dtype=bool))
        scores = jnp.where(causal, scores, -jnp.inf)
        attn = jax.nn.softmax(scores, axis=-1)
        out = jnp.einsum('bhqk,bhkd->bhqd', attn, v)
        out = out.transpose(0, 2, 1, 3).reshape(B, S, D)
        return out @ Wo.T + bo

    def _L0_ffn_ref(x, W1, W2, W3):
        import jax, jax.numpy as jnp
        import numpy as np
        B, S, D, H = (4, 256, 256, 1024)

        def fwht(x):
            orig_shape = x.shape
            n = orig_shape[-1]
            x = x.reshape(-1, n)
            h = 1
            while h < n:
                xb = x.reshape(-1, n // (2 * h), 2, h)
                a = xb[:, :, 0, :]
                b = xb[:, :, 1, :]
                x = jnp.stack([a + b, a - b], axis=2).reshape(-1, n)
                h *= 2
            scale = jnp.asarray(1.0 / np.sqrt(n), dtype=x.dtype)
            return (x * scale).reshape(orig_shape)
        up_gate = jnp.einsum('bsd,hd->bsh', x, W1)
        up_lin = jnp.einsum('bsd,hd->bsh', x, W3)
        hidden = jax.nn.silu(up_gate) * up_lin
        hidden = fwht(hidden)
        out = jnp.einsum('bsh,dh->bsd', hidden, W2)
        return out
    x = L0_attn_x
    x = x + _layernorm(_L0_attn_ref(_layernorm(x, axis=-1), L0_attn_Wq, L0_attn_Wk, L0_attn_Wv, L0_attn_Wo, L0_attn_bo), axis=-1)
    x = x + _layernorm(_L0_ffn_ref(_layernorm(x, axis=-1), L0_ffn_W1, L0_ffn_W2, L0_ffn_W3), axis=-1)
    return x

_drawn_inputs = setup_inputs


def setup_inputs(seed=0):
    import zlib

    import numpy as np

    out = dict(_drawn_inputs(seed))
    spreads = {}
    factors = {}
    for name, (base, spread) in spreads.items():
        noise = np.random.default_rng([zlib.crc32(name.encode()), seed]).standard_normal(out[name].shape)
        drawn = base * np.exp(spread * noise) if base else spread * noise
        out[name] = jnp.asarray(drawn.astype(out[name].dtype))
    for name, factor in factors.items():
        out[name] = (out[name] * factor).astype(out[name].dtype)
    return out
```

```python
from contextlib import ExitStack

import concourse.bass as bass
from concourse import mybir

F32 = mybir.dt.float32
F32R = mybir.dt.float32r
BF16 = mybir.dt.bfloat16
ALU = mybir.AluOpType
ACT = mybir.ActivationFunctionType
AX = mybir.AxisListType

P = 128
B, S, D, H = 4, 1024, 256, 1024
HEADS, DH = 16, 16
HG = 4
KC = D // P
QT = 256
NQ = B * S // QT
NT = B * HEADS // HG
EPS = 1e-5
SCALE = 0.25
NEG = -1e30
CH = 512
LEAD = 16

STEPS = [(c, kb) for c in range(S // CH) for kb in range(4 * c + 4)]
PIECES = [(p, i, r) for p in range(2) for i in range(S // P) for r in range(1 if i < 4 else 2)]
NS, NM = len(STEPS), len(PIECES)
M_AT = [0, 3, 3, 3, 3, 3, 3, 2, 2, 2, 0, 0]
M_FROM = [sum(M_AT[:s]) for s in range(NS)]
NF = H // P

X_USE = {
    (1, 1): ("attn", 0), (3, 0): ("lnT", 0), (4, 0): ("ln2T", 0), (4, 1): ("qk", 0), (5, 0): ("ffn", 0),
    (5, 1): ("qk", 1), (6, 0): ("v", 0), (6, 1): ("ffn", 1), (7, 0): ("ffn", 2), (7, 1): ("ffn", 3),
    (8, 0): ("ffn", 4), (8, 1): ("ffn", 5), (9, 0): ("ffn", 6), (9, 1): ("ffn", 7), (10, 0): ("maxT", 0),
    (11, 0): ("down", 0),
}
FRONT_USES = [("lnT", 0), ("qk", 0), ("qk", 1), ("v", 0)]


def uses_of(front, maxima, back):
    kinds = {"lnT": front, "qk": front, "v": front, "maxT": maxima,
             "attn": back, "ln2T": back, "ffn": back, "down": back}
    return [X_USE[k] for k in sorted(X_USE) if kinds[X_USE[k][0]]]


def diagonal(s):
    c, kb = STEPS[s]
    return kb >= 4 * c


def span(s):
    c, kb = STEPS[s]
    q0 = max(CH * c, P * kb)
    return q0, CH * (c + 1) - q0


def piece(k):
    p, i, r = PIECES[k]
    k0 = 512 * r
    w = min(512, P * (i + 1) - k0)
    return p, i, r, k0, w, k0 + w == P * (i + 1)


def block(nc, x, wqT, wkT, wvT, woT, bo, w1T, w3T, w2T, had, ident, upper, out):
    ctx = ExitStack()
    with ctx:
        def sb(name, shape, dt=F32):
            return ctx.enter_context(nc.sbuf_tensor(name, shape, dt))

        def sem(name):
            return ctx.enter_context(nc.semaphore(name))

        qk_dram = nc.dram_tensor("qk_scratch", [B, 2, HEADS, 2, DH, S], F32).ap()
        o_dram = nc.dram_tensor("o_scratch", [NQ, D, QT], F32).ap()

        identF = sb("identF", [P, P])
        hadF = sb("hadF", [P, P])
        upF = sb("upF", [P, P])
        identB = sb("identB", [P, P], BF16)
        maskB = sb("maskB", [P, P], BF16)
        mhalf = sb("mhalf", [P, 2])
        wqk = [sb(f"wqk_{n}", [P, KC, 2 * D], F32R) for n in ("hi", "lo")]
        wv = [sb(f"wv_{n}", [P, KC, D], F32R) for n in ("hi", "lo")]
        wo = sb("wo", [P, KC, D])
        bo_row = sb("bo_row", [1, D])
        bo_r = [sb(f"bo_{n}", [1, D], F32R) for n in ("hi", "lo")]
        ones = sb("ones", [1, P], F32R)
        w13 = [sb(f"w13_{n}", [P, 2, KC, H], F32R) for n in ("hi", "lo")]
        w2 = [sb(f"w2_{n}", [P, NF, D], F32R) for n in ("hi", "lo")]
        spare = sb("spare", [P, 2])
        spare_p = sb("spare_p", [P, NS + 1])
        xa = sb("xa", [P, 2, D])
        xn = sb("xn", [P, 2, D])
        xT = [sb(f"xT_{n}", [P, KC, QT], F32R) for n in ("hi", "lo")]
        qk = [sb(f"qk_{n}", [P, 4, QT], F32R) for n in ("hi", "lo")]
        v_all = sb("v_all", [P, 2 * S // P, D])
        Qs = [sb(f"Qs{i}", [P, 2, S], F32R) for i in range(2)]
        Ks = [sb(f"Ks{i}", [P, 2, S], F32R) for i in range(2)]
        Vg = [sb(f"Vg{i}", [P, S // P, HG, 32]) for i in range(2)]
        Pt = sb("Pt", [P, 2, HG, CH])
        m0 = sb("m0", [P, HG, 8])
        m1 = sb("m1", [P, HG, 4])
        mrow = [sb(f"mrow_{n}", [32, P], F32R) for n in ("hi", "lo")]
        den = sb("den", [P, CH])
        rec = sb("rec", [P, CH])
        On = sb("On", [P, 2, CH])
        work = sb("work", [P, 8, 512])
        xc, oc, an, x1, xn2, yo = (work[:, i, :].rearrange("p (j d) -> p j d", j=2) for i in range(6))
        th = work[:, 6, :].rearrange("p (j d) -> p j d", j=2)
        hf = work[:, 7, :].rearrange("p (j d) -> p j d", j=2)
        hw = sb("hw", [P, QT])
        nT = [sb(f"nT_{n}", [P, KC, QT], F32R) for n in ("hi", "lo")]
        hh = [sb(f"hh_{n}", [P, NF, QT], F32R) for n in ("hi", "lo")]
        st6 = sb("st6", [P, 4, 2, 6])
        mv = sb("mv", [P, 4, 2, 2])
        ve = sb("ve", [P, 4, 2])
        rs = sb("rs", [P, 4, 2])
        nmr = sb("nmr", [P, 4, 2])
        raw = Pt[:].rearrange("p a h q -> p (a h q)")
        flat = work[:].rearrange("p a q -> p (a q)")
        raw_q, raw_k, raw_v = (raw[:, i * 512:(i + 1) * 512].rearrange("p (k n) -> p k n", k=KC) for i in range(3))
        raw_w2 = raw[:, 2048:4096].rearrange("p (c n) -> p c n", c=NF)
        had_a = flat[:, 0:2048].rearrange("p (c n) -> p c n", c=NF)
        had_b = flat[:, 2048:4096].rearrange("p (c n) -> p c n", c=NF)
        raw_w13 = flat.rearrange("p (m k n) -> p m k n", m=2, k=KC)

        Sp = ctx.enter_context(nc.psum_tensor("Sp", [P, 4, 512], F32))
        Mp = ctx.enter_context(nc.psum_tensor("Mp", [P, 2, 512], F32))
        Vp = ctx.enter_context(nc.psum_tensor("Vp", [P, 512], F32))
        Xp = ctx.enter_context(nc.psum_tensor("Xp", [P, 512], F32))
        X2 = Xp[:, :].rearrange("p (j d) -> p j d", j=2)

        consts_in = sem("consts_in")
        proj_in = sem("proj_in")
        w2_in = sem("w2_in")
        w13_in = sem("w13_in")
        small_set = sem("small_set")
        spare_set = sem("spare_set")
        bf_set = sem("bf_set")
        hi_set = sem("hi_set")
        lo_set = sem("lo_set")
        had_done = sem("had_done")
        had_out = sem("had_out")
        fly = sem("fly")
        w2_hi = sem("w2_hi")
        w2_set = sem("w2_set")
        w13_hi = sem("w13_hi")
        w13_set = sem("w13_set")
        xa_in = sem("xa_in")
        a_st, a_mv, a_ve, a_rs, a_xn = (sem(n) for n in ("a_st", "a_mv", "a_ve", "a_rs", "a_xn"))
        a_T, a_hi, a_lo = sem("a_T"), sem("a_hi"), sem("a_lo")
        a_qk, a_qkhi, a_qklo = sem("a_qk"), sem("a_qkhi"), sem("a_qklo")
        qk_out = sem("qk_out")
        a_v, a_vout = sem("a_v"), sem("a_vout")
        stacked = sem("stacked")
        vg_set = sem("vg_set")
        m_full, m_red = sem("m_full"), sem("m_red")
        m_all, m_T, m_hi, m_lo = sem("m_all"), sem("m_T"), sem("m_hi"), sem("m_lo")
        mrow_in = sem("mrow_in")
        s_full, exp_done = sem("s_full"), sem("exp_done")
        p_masked = sem("p_masked")
        pv_done = sem("pv_done")
        n_den, n_rec, n_out = sem("n_den"), sem("n_rec"), sem("n_out")
        o_out = [sem(f"o_out{c}") for c in range(2)]
        xc_in, oc_in = sem("xc_in"), sem("oc_in")
        c_attn, c_down = sem("c_attn"), sem("c_down")
        c_st, c_mv, c_ve, c_rs = (sem(n) for n in ("c_st", "c_mv", "c_ve", "c_rs"))
        c_nmr = sem("c_nmr")
        c_an, c_x1, c_xn2 = sem("c_an"), sem("c_x1"), sem("c_xn2")
        c_T, c_hi, c_lo = sem("c_T"), sem("c_hi"), sem("c_lo")
        f_gu, f_th, f_w, f_h, f_hi, f_lo = (sem(n) for n in ("f_gu", "f_th", "f_w", "f_h", "f_hi", "f_lo"))
        c_yn, c_y, y_out = sem("c_yn"), sem("c_y"), sem("y_out")

        x_rows = x.rearrange("b (q j p) d -> (b q) p j d", j=2, p=P)
        out_rows = out.rearrange("b (q j p) d -> (b q) p j d", j=2, p=P)

        blk = ctx.enter_context(nc.Block())

        @blk.sync
        def _(sp):
            def load_xa(a, first=False):
                if not first:
                    sp.wait_ge(a_xn, a)
                sp.dma_start(xa[:], x_rows[a]).then_inc(xa_in, 16)

            def store_qk(a):
                sp.wait_ge(a_qkhi, 2 * a + 2)
                sp.wait_ge(a_qklo, 2 * a + 2)
                bb, q0 = a // 4, (a % 4) * QT
                for m in range(4):
                    for half in range(2):
                        sp.dma_start(qk_dram[bb, m // 2, 8 * (m % 2):8 * (m % 2) + 8, half, :, bass.ds(q0, QT)],
                                     qk[half][:, m, :].bitcast(F32)).then_inc(qk_out, 16)

            def stack(t, par, quarters, first=False):
                bb, h0 = t // 4, (t % 4) * HG
                if quarters:
                    sp.wait_ge(qk_out, LEAD + 128 * quarters)
                if first:
                    sp.wait_ge(small_set, 1)
                else:
                    sp.wait_ge(s_full, LEAD + 2 * NS * (t - 1))
                for h in range(HG):
                    row, p = 64 * (h % 2), h // 2
                    both = lambda n: qk_dram[bb, n, h0 + h].rearrange("a r t -> (a r) t")
                    high = lambda n: qk_dram[bb, n, h0 + h, 0]
                    sp.dma_start(Qs[par][row:row + 32, p, :].bitcast(F32), both(0)).then_inc(stacked, 16)
                    sp.dma_start(Qs[par][row + 32:row + 48, p, :].bitcast(F32), high(0)).then_inc(stacked, 16)
                    sp.dma_start(Ks[par][row:row + 16, p, :].bitcast(F32), high(1)).then_inc(stacked, 16)
                    sp.dma_start(Ks[par][row + 16:row + 48, p, :].bitcast(F32), both(1)).then_inc(stacked, 16)

            def maxima_rows(t, par, front=False):
                sp.wait_ge(m_hi, t + 1)
                sp.wait_ge(m_lo, t + 1)
                for h in range(HG):
                    for half in range(2):
                        row = 64 * (h % 2) + 48 + half
                        if front and h == 3 and half == 1:
                            sp.wait_ge(qk_out, LEAD + 128 * (t + 6))
                        sp.dma_start(Qs[par][row:row + 1, h // 2, :].bitcast(F32),
                                     mrow[half][8 * h:8 * h + 8, :].bitcast(F32)).then_inc(mrow_in, 16)

            def store_o(t, c):
                sp.wait_ge(n_out, LEAD + 2 * t + c + 1)
                bb, g = t // 4, t % 4
                for h in range(HG):
                    sp.dma_start(o_dram[bass.ds(4 * bb + 2 * c, 2), bass.ds(64 * g + DH * h, DH), :]
                                 .rearrange("q r t -> r q t"),
                                 On[32 * h:32 * h + DH, c, :].rearrange("p (q t) -> p q t", q=2))\
                      .then_inc(o_out[c], 16)

            def load_back(c, units_stored):
                sp.wait_ge(c_x1, LEAD + c)
                sp.dma_start(xc, x_rows[c]).then_inc(xc_in, 16)
                for o in o_out:
                    sp.wait_ge(o, LEAD + 64 * units_stored)
                sp.wait_ge(c_attn, LEAD + c)
                sp.dma_start(oc, o_dram[c].rearrange("(k p) t -> p k t", p=P)).then_inc(oc_in, 16)

            def store_y(c):
                sp.wait_ge(c_y, LEAD + c + 1)
                sp.dma_start(out_rows[c], yo).then_inc(y_out, 16)

            def body(t, par, maxima, front, back):
                if maxima:
                    stack(t + 1, (par + 1) % 2, None if front else NQ)
                if front:
                    load_xa(t + 6)
                if back:
                    load_back(t - 4, t)
                store_o(t, 0)
                if front:
                    store_qk(t + 6)
                if maxima:
                    maxima_rows(t + 1, (par + 1) % 2, front)
                store_o(t, 1)
                if back:
                    store_y(t - 4)

            for lead in (s_full, c_x1, c_attn, a_vout, n_out, c_yn, a_v, qk_out, f_gu, c_down, c_y, a_T, c_T, f_lo,
                         y_out, *o_out):
                sp.sem_inc(lead, LEAD)
            sp.dma_start(xa[:], x_rows[0]).then_inc(xa_in, 16)
            for dst, src in ((raw_q, wqT), (raw_k, wkT), (raw_v, wvT)):
                sp.dma_start(dst, src.rearrange("(k p) n -> p k n", p=P)).then_inc(proj_in, 16)
            for dst, src in ((identF[:], ident), (hadF[:], had), (upF[:], upper),
                             (wo[:], woT.rearrange("(k p) n -> p k n", p=P)), (bo_row[:], bo.rearrange("(o n) -> o n", o=1))):
                sp.dma_start(dst, src).then_inc(consts_in, 16)
            sp.dma_start(raw_w2, w2T.rearrange("(c p) n -> p c n", p=P)).then_inc(w2_in, 16)
            store_qk(0)
            with sp.Fori(1, 6) as a:
                load_xa(a)
                store_qk(a)
            stack(0, 0, 6, first=True)
            maxima_rows(0, 0)
            sp.wait_ge(w2_set, 1)
            for m, src in enumerate((w1T, w3T)):
                sp.dma_start(raw_w13[:, m], src.rearrange("(k p) n -> p k n", p=P)).then_inc(w13_in, 16)
            with sp.Fori(0, 2) as i:
                for par in range(2):
                    body(2 * i + par, par, True, True, False)
            sp.wait_ge(w13_set, 1)
            with sp.Fori(2, 5) as i:
                for par in range(2):
                    body(2 * i + par, par, True, True, True)
            with sp.Fori(5, 7) as i:
                for par in range(2):
                    body(2 * i + par, par, True, False, True)
            body(14, 0, True, False, True)
            body(15, 1, False, False, True)
            with sp.Fori(NQ - 4, NQ) as c:
                load_back(c, NT)
                store_y(c)
            sp.wait_ge(y_out, LEAD + 16 * NQ)
            sp.wait_ge(qk_out, LEAD + 16 * 8 * NQ)
            for o in o_out:
                sp.wait_ge(o, LEAD + 64 * NT)

        @blk.tensor
        def _(pe):
            def split_products(dst, left, right, lcols, rcols, k_chunks):
                n = 0
                for lh, rh in ((0, 0), (0, 1), (1, 0)):
                    for k in range(k_chunks):
                        mm = nc.tensor.matmul(dst, left[lh][:, k, lcols], right[rh][:, k, rcols],
                                              start=(n == 0), stop=(n == 3 * k_chunks - 1))
                        n += 1
                return mm

            def x_read(kind, j, a, t, c):
                done, count = {"lnT": (a_lo, lambda: a + 1), "qk": (a_qklo, lambda: 2 * a + j + 1),
                               "v": (a_vout, lambda: LEAD + a + 1), "maxT": (m_lo, lambda: t + 1),
                               "attn": (c_an, lambda: c + 1), "ln2T": (c_lo, lambda: c + 1),
                               "ffn": (f_h, lambda: 8 * c + j + 1), "down": (c_yn, lambda: LEAD + c + 1)}[kind]
                pe.wait_ge(done, count())

            def x_use(kind, j, a, t, c):
                if kind == "lnT":
                    pe.wait_ge(a_xn, a + 1)
                    for k in range(KC):
                        for i in range(2):
                            mm = nc.tensor.transpose(Xp[:, k * QT + i * P:k * QT + (i + 1) * P],
                                                     xn[:, i, k * P:(k + 1) * P], identF[:])
                    mm.then_inc(a_T, 1)
                elif kind == "qk":
                    pe.wait_ge(a_hi, a + 1)
                    pe.wait_ge(a_lo, a + 1)
                    for i in range(2):
                        m = 2 * j + i
                        mm = split_products(Xp[:, i * QT:(i + 1) * QT], wqk, xT, slice(m * P, (m + 1) * P),
                                            slice(0, QT), KC)
                    mm.then_inc(a_qk, 1)
                elif kind == "v":
                    for i in range(2):
                        mm = split_products(Xp[:, i * D:(i + 1) * D], xT, wv, slice(i * P, (i + 1) * P),
                                            slice(0, D), KC)
                    mm.then_inc(a_v, 1)
                elif kind == "maxT":
                    pe.wait_ge(m_all, t + 1)
                    nc.tensor.transpose(Xp[0:32, 0:P], m0[:].rearrange("p h i -> p (h i)"), identF[:])\
                      .then_inc(m_T, 1)
                elif kind == "attn":
                    pe.wait_ge(oc_in, 16 * (c + 1))
                    for i in range(2):
                        dst = Xp[:, i * D:(i + 1) * D]
                        for k in range(KC):
                            nc.tensor.matmul(dst, oc[:, k, i * P:(i + 1) * P], wo[:, k, :], start=(k == 0), stop=False)
                        for half in range(2):
                            mm = nc.tensor.matmul(dst, ones[0:1, :], bo_r[half][0:1, :], start=False, stop=(half == 1))
                    mm.then_inc(c_attn, 1)
                elif kind == "ln2T":
                    pe.wait_ge(c_xn2, c + 1)
                    for k in range(KC):
                        for i in range(2):
                            mm = nc.tensor.transpose(Xp[:, k * QT + i * P:k * QT + (i + 1) * P],
                                                     xn2[:, i, k * P:(k + 1) * P], identF[:])
                    mm.then_inc(c_T, 1)
                elif kind == "ffn":
                    if j == 0:
                        pe.wait_ge(c_hi, c + 1)
                        pe.wait_ge(c_lo, c + 1)
                    for m in range(2):
                        w = [w13[h][:, m] for h in range(2)]
                        mm = split_products(Xp[:, m * QT:(m + 1) * QT], w, nT, slice(j * P, (j + 1) * P),
                                            slice(0, QT), KC)
                    mm.then_inc(f_gu, 1)
                elif kind == "down":
                    pe.wait_ge(f_hi, 8 * c + 8)
                    pe.wait_ge(f_lo, LEAD + 8 * c + 8)
                    for i in range(2):
                        mm = split_products(Xp[:, i * D:(i + 1) * D], hh, w2, slice(i * P, (i + 1) * P),
                                            slice(0, D), NF)
                    mm.then_inc(c_down, 1)

            def max_piece(t, par, k):
                p, i, r, k0, w, diag = piece(k)
                if k == 0:
                    pe.wait_ge(stacked, 256 * (t + 1))
                pe.wait_ge(m_red, NM * t + k)
                for half in range(2):
                    lo = 64 * half
                    mm = nc.tensor.matmul(Mp[:, half, 0:w], Qs[par][lo:lo + 48, p, i * P:(i + 1) * P],
                                          Ks[par][lo:lo + 48, p, k0:k0 + w], start=True, stop=not diag)
                if diag:
                    for half in range(2):
                        mm = nc.tensor.matmul(Mp[:, half, w - P:w], identB[:], maskB[:], start=False, stop=True)
                mm.then_inc(m_full, 1)

            def scores(t, par, s, p):
                c, kb = STEPS[s]
                q0, n = span(s)
                if s == 0 and p == 0:
                    pe.wait_ge(mrow_in, 128 * (t + 1))
                pe.wait_ge(exp_done, 2 * NS * t + 2 * s + p + 1)
                for half in range(2):
                    lo = 64 * half
                    mm = nc.tensor.matmul(Sp[:, 2 * p + half, 0:n], Ks[par][lo:lo + 50, p, kb * P:(kb + 1) * P],
                                          Qs[par][lo:lo + 50, p, q0:q0 + n], start=True, stop=True)
                mm.then_inc(s_full, 1)

            def pv(t, par, s):
                c, kb = STEPS[s]
                q0, n = span(s)
                if s == 0:
                    pe.wait_ge(vg_set, t + 1)
                if kb == 0:
                    pe.wait_ge(n_out, LEAD + 2 * t + c)
                if diagonal(s):
                    pe.wait_ge(p_masked, 8 * t + 4 * c + kb - 4 * c + 1)
                else:
                    pe.wait_ge(exp_done, 2 * NS * t + 2 * s + 4)
                for h in range(HG):
                    mm = nc.tensor.matmul(Vp[32 * h:32 * h + 32, CH - n:CH], Vg[par][:, kb, h, :],
                                          Pt[:, s % 2, h, 0:n], start=(kb == 0), stop=(kb == 4 * c + 3))
                mm.then_inc(pv_done, 1)

            def body(t, par, second, maxima, front, back):
                used = uses_of(front, maxima, back)
                before = None
                for s in range(NS):
                    m = list(range(M_FROM[s], M_FROM[s] + M_AT[s])) if maxima else []
                    for place in range(2):
                        if len(m) > place:
                            max_piece(t + 1, (par + 1) % 2, m[place])
                        if second:
                            scores(t, par, s, place)
                        u = X_USE.get((s, place))
                        if u in used:
                            if before:
                                x_read(*before, t + 6, t + 1, t - 4)
                            else:
                                if second:
                                    pe.wait_ge(m_lo, t + 1)
                                if back:
                                    pe.wait_ge(c_yn, LEAD + t - 4)
                            x_use(*u, t + 6, t + 1, t - 4)
                            before = u
                    if len(m) > 2:
                        max_piece(t + 1, (par + 1) % 2, m[2])
                    if second and s:
                        pv(t, par, s - 1)
                if second:
                    pv(t, par, NS - 1)

            pe.wait_ge(consts_in, 16 * 5)
            pe.wait_ge(hi_set, 4)
            pe.wait_ge(lo_set, 4)
            pe.wait_ge(small_set, 1)
            with pe.Fori(0, 6) as a:
                pe.wait_ge(a_vout, LEAD + a)
                for n, u in enumerate(FRONT_USES):
                    if n:
                        x_read(*FRONT_USES[n - 1], a, None, None)
                    x_use(*u, a, None, None)
            pe.wait_ge(bf_set, 2)
            for k in range(NM):
                max_piece(0, 0, k)
            pe.wait_ge(a_vout, LEAD + 6)
            x_use("maxT", 0, None, 0, None)
            pe.wait_ge(w2_in, 16)
            for c in range(NF):
                mm = nc.tensor.matmul(Sp[:, c // 2, (c % 2) * D:(c % 2 + 1) * D], hadF[:], raw_w2[:, c, :],
                                      start=True, stop=True)
            mm.then_inc(had_done, 1)
            pe.wait_ge(had_out, 1)
            with pe.Fori(0, 2) as i:
                for par in range(2):
                    body(2 * i + par, par, True, True, True, False)
            pe.wait_ge(w13_set, 1)
            with pe.Fori(2, 5) as i:
                for par in range(2):
                    body(2 * i + par, par, True, True, True, True)
            with pe.Fori(5, 7) as i:
                for par in range(2):
                    body(2 * i + par, par, True, True, False, True)
            body(14, 0, True, True, False, True)
            body(15, 1, True, False, False, True)
            with pe.Fori(16, 20) as t:
                body(t, 0, False, False, False, True)

        @blk.scalar
        def _(act):
            def copy(dst, src, **kw):
                return nc.scalar.activation(dst, src, ACT.Copy, **kw)

            def x_reader(kind, j, a, t, c, reused=True):
                if kind == "lnT":
                    act.wait_ge(a_T, LEAD + a + 1)
                    act.wait_ge(a_v, LEAD + a)
                    copy(xT[0][:].rearrange("p k t -> p (k t)"), Xp[:, :]).then_inc(a_hi, 1)
                elif kind == "qk":
                    act.wait_ge(a_qk, 2 * a + j + 1)
                    act.wait_ge(qk_out, LEAD + 128 * a)
                    copy(qk[0][:, 2 * j:2 * j + 2, :], X2).then_inc(a_qkhi, 1)
                elif kind == "v":
                    act.wait_ge(a_v, LEAD + a + 1)
                    if reused:
                        act.wait_ge(vg_set, a - 4)
                    copy(v_all[:, bass.ds(2 * (a % 8), 2), :], X2).then_inc(a_vout, 1)
                elif kind == "maxT":
                    act.wait_ge(m_T, t + 1)
                    act.wait_ge(mrow_in, 128 * t)
                    copy(mrow[0][:], Xp[0:32, 0:P]).then_inc(m_hi, 1)
                elif kind == "ln2T":
                    act.wait_ge(c_T, LEAD + c + 1)
                    act.wait_ge(f_gu, LEAD + 8 * c)
                    copy(nT[0][:].rearrange("p k t -> p (k t)"), Xp[:, :]).then_inc(c_hi, 1)
                elif kind == "ffn":
                    act.wait_ge(f_gu, LEAD + 8 * c + j + 1)
                    nc.scalar.activation(th[:, j % 2, :], Xp[:, 0:QT], ACT.Tanh, scale=0.5).then_inc(f_th, 1)
                    if j:
                        hidden_hi(c, j - 1)

            def hidden_hi(c, j):
                act.wait_ge(f_h, 8 * c + j + 1)
                act.wait_ge(c_down, LEAD + c)
                copy(hh[0][:, j, :], hf[:, j % 2, :]).then_inc(f_hi, 1)

            def normalise(c, which):
                act.wait_ge(c_nmr, 2 * c + which + 1)
                if which == 0:
                    act.wait_ge(c_x1, LEAD + c)
                else:
                    act.wait_ge(c_y, LEAD + c)
                n = 1 + 2 * which
                dst = an if which == 0 else yn
                for i in range(2):
                    last = nc.scalar.activation(dst[:, i, :], X2[:, i, :], ACT.Identity, bias=nmr[:, n, i:i + 1],
                                                scale=rs[:, n, i:i + 1])
                last.then_inc(c_an if which == 0 else c_yn, 1)

            def exps(t, s, p):
                _, n = span(s)
                act.wait_ge(s_full, LEAD + 2 * NS * t + 2 * s + p + 1)
                act.wait_ge(pv_done, NS * t + s + 1)
                nc.scalar.activation(Pt[:, s % 2, 2 * p:2 * p + 2, 0:n], Sp[:, 2 * p:2 * p + 2, 0:n], ACT.Exp,
                                     scale=SCALE).then_inc(exp_done, 1)

            yn = an

            def body(t, second, maxima, front, back):
                used = uses_of(front, maxima, back)
                for s in range(NS):
                    if back and s == 10:
                        hidden_hi(t - 4, 7)
                    for place in range(2):
                        if second:
                            exps(t, s, place)
                        u = X_USE.get((s, place))
                        if u in used:
                            x_reader(*u, t + 6, t + 1, t - 4)
                    if back and s == 2:
                        normalise(t - 4, 0)
                    if back and s == 11:
                        normalise(t - 4, 1)

            act.wait_ge(proj_in, 48)
            copy(wqk[0][:, :, 0:D], raw_q).then_inc(hi_set, 1)
            copy(wqk[0][:, :, D:2 * D], raw_k).then_inc(hi_set, 1)
            copy(wv[0][:], raw_v).then_inc(hi_set, 1)
            act.wait_ge(consts_in, 16 * 5)
            copy(bo_r[0][:], bo_row[:]).then_inc(hi_set, 1)
            with act.Fori(0, 6) as a:
                for u in FRONT_USES:
                    x_reader(*u, a, None, None, reused=False)
            x_reader("maxT", 0, None, 0, None)
            act.wait_ge(had_done, 1)
            copy(flat[:, 0:2048], Sp[:].rearrange("p b n -> p (b n)"), scale=1.0 / 64).then_inc(had_out, 1)
            act.wait_ge(fly, 12)
            copy(w2[0][:], had_b).then_inc(w2_hi, 1)
            with act.Fori(0, 2) as i:
                for par in range(2):
                    body(2 * i + par, True, True, True, False)
            act.wait_ge(w13_in, 32)
            copy(w13[0][:], raw_w13).then_inc(w13_hi, 1)
            with act.Fori(2, 5) as i:
                for par in range(2):
                    body(2 * i + par, True, True, True, True)
            with act.Fori(5, 7) as i:
                for par in range(2):
                    body(2 * i + par, True, True, False, True)
            body(14, True, True, False, True)
            body(15, True, False, False, True)
            with act.Fori(16, 20) as t:
                body(t, False, False, False, True)

        @blk.vector
        def _(dve):
            def minus_hi(dst, src, hi):
                return nc.vector.tensor_tensor(dst, src, hi.bitcast(F32), ALU.subtract)

            def stats(n, src, k, s_st, s_mv, s_ve):
                for i in range(2):
                    last = nc.vector.bn_stats(st6[:, n, i, :], src[:, i, :])
                last.then_inc(s_st, 1)
                dve.wait_ge(s_st, k + 1)
                nc.vector.memset(spare[0:1, 0:1], 0.0)
                for i in range(2):
                    last = nc.vector.bn_aggr(mv[:, n, i, :], st6[:, n, i, :])
                last.then_inc(s_mv, 1)
                dve.wait_ge(s_mv, k + 1)
                nc.vector.tensor_scalar(ve[:, n, :], mv[:, n, :, 1], EPS, None, ALU.add).then_inc(s_ve, 1)

            def apply_ln(n, dst, src, done):
                for i in range(2):
                    last = nc.vector.tensor_scalar(dst[:, i, :], src[:, i, :], mv[:, n, i, 0:1], rs[:, n, i:i + 1],
                                                   ALU.subtract, ALU.mult)
                last.then_inc(done, 1)

            def front_stats(a):
                dve.wait_ge(xa_in, 16 * (a + 1))
                stats(0, xa, a, a_st, a_mv, a_ve)

            def front_ln(a):
                dve.wait_ge(a_rs, a + 1)
                dve.wait_ge(a_T, LEAD + a)
                apply_ln(0, xn, xa, a_xn)

            def shift(n, c, which):
                dve.wait_ge(c_rs, 3 * c + n)
                nc.vector.scalar_tensor_tensor(nmr[:, n, :], mv[:, n, :, 0], -1.0, rs[:, n, :], ALU.mult, ALU.mult)\
                  .then_inc(c_nmr, 1)

            def back_ln2(c):
                dve.wait_ge(c_rs, 3 * c + 2)
                dve.wait_ge(c_T, LEAD + c)
                apply_ln(2, xn2, x1, c_xn2)

            def x_reader(kind, j, a, t, c):
                if kind == "lnT":
                    dve.wait_ge(a_hi, a + 1)
                    minus_hi(xT[1][:].rearrange("p k t -> p (k t)"), Xp[:, :], xT[0][:].rearrange("p k t -> p (k t)"))\
                        .then_inc(a_lo, 1)
                elif kind == "qk":
                    dve.wait_ge(a_qkhi, 2 * a + j + 1)
                    minus_hi(qk[1][:, 2 * j:2 * j + 2, :], X2, qk[0][:, 2 * j:2 * j + 2, :])\
                        .then_inc(a_qklo, 1)
                elif kind == "maxT":
                    dve.wait_ge(m_hi, t + 1)
                    minus_hi(mrow[1][:], Xp[0:32, 0:P], mrow[0][:]).then_inc(m_lo, 1)
                elif kind == "ln2T":
                    dve.wait_ge(c_hi, c + 1)
                    minus_hi(nT[1][:].rearrange("p k t -> p (k t)"), Xp[:, :], nT[0][:].rearrange("p k t -> p (k t)"))\
                        .then_inc(c_lo, 1)
                elif kind == "ffn":
                    dve.wait_ge(f_th, 8 * c + j + 1)
                    nc.vector.scalar_tensor_tensor(hw[:], th[:, j % 2, :], 1.0, Xp[:, 0:QT], ALU.add, ALU.mult)\
                      .then_inc(f_w, 1)
                    dve.wait_ge(f_w, 8 * c + j + 1)
                    if j >= 2:
                        dve.wait_ge(f_lo, LEAD + 8 * c + j - 1)
                    else:
                        dve.wait_ge(f_lo, LEAD + 8 * c)
                    nc.vector.tensor_tensor(hf[:, j % 2, :], hw[:], Xp[:, QT:2 * QT], ALU.mult)\
                      .then_inc(f_h, 1)

            def reduce_piece(t, k):
                p, i, r, k0, w, diag = piece(k)
                if k == 0:
                    dve.wait_ge(m_T, t)
                dve.wait_ge(m_full, NM * t + k + 1)
                dst = m0[:, 2 * p:2 * p + 2, i] if r == 0 else m1[:, 2 * p:2 * p + 2, i - 4]
                nc.vector.tensor_reduce(dst, Mp[:, :, 0:w], AX.X, ALU.max, negate=True).then_inc(m_red, 1)

            def join_maxima(t):
                dve.wait_ge(m_red, NM * (t + 1))
                nc.vector.tensor_tensor(m0[:, :, 4:8], m0[:, :, 4:8], m1[:], ALU.min).then_inc(m_all, 1)

            def normalise_o(t, c):
                dve.wait_ge(pv_done, NS * t + 4 + 8 * c + 2)
                nc.vector.memset(spare[0:1, 0:1], 0.0)
                nc.vector.stream_shuffle(den[:], Vp[:, :], [16] * 32).then_inc(n_den, 1)
                dve.wait_ge(n_den, 2 * t + c + 1)
                nc.vector.reciprocal(rec[:], den[:]).then_inc(n_rec, 1)
                dve.wait_ge(n_rec, 2 * t + c + 1)
                dve.wait_ge(o_out[c], LEAD + 64 * t)
                nc.vector.tensor_tensor(On[:, c, :], Vp[:, :], rec[:], ALU.mult).then_inc(n_out, 1)

            def body(t, second, maxima, front, back):
                used = uses_of(front, maxima, back)
                for s in range(NS):
                    m = list(range(M_FROM[s], M_FROM[s] + M_AT[s])) if maxima else []
                    if back and s == 2:
                        dve.wait_ge(c_attn, LEAD + t - 4 + 1)
                        stats(1, X2, 3 * (t - 4), c_st, c_mv, c_ve)
                    if back and s == 3:
                        dve.wait_ge(c_x1, LEAD + t - 4 + 1)
                        stats(2, x1, 3 * (t - 4) + 1, c_st, c_mv, c_ve)
                    if front and s == 1:
                        front_stats(t + 6)
                    for place in range(2):
                        if len(m) > place:
                            reduce_piece(t + 1, m[place])
                        if place == 0 and back and s == 2:
                            shift(1, t - 4, 0)
                        u = X_USE.get((s, place))
                        if u in used:
                            x_reader(*u, t + 6, t + 1, t - 4)
                    if len(m) > 2:
                        reduce_piece(t + 1, m[2])
                    if front and s == 2:
                        front_ln(t + 6)
                    if back and s == 3:
                        back_ln2(t - 4)
                    if maxima and s == 9:
                        join_maxima(t + 1)
                    if second and s == 4:
                        normalise_o(t, 0)
                    if back and s == 11:
                        dve.wait_ge(c_down, LEAD + t - 4 + 1)
                        stats(3, X2, 3 * (t - 4) + 2, c_st, c_mv, c_ve)
                        shift(3, t - 4, 1)
                if second:
                    normalise_o(t, 1)

            nc.vector.memset(mhalf[:], -0.5)
            nc.vector.memset(ones[:].bitcast(F32), 1.0)
            for i in range(2):
                nc.vector.memset(Ks[i][32:64, :, :].bitcast(F32), 1.0)
                nc.vector.memset(Ks[i][96:128, :, :].bitcast(F32), 1.0)
                nc.vector.memset(Vg[i][:, :, :, DH:32], 1.0)
            nc.vector.memset(spare[:, 0:1], 0.0).then_inc(exp_done, 2)
            nc.vector.memset(spare[:, 1:2], 0.0).then_inc(pv_done, 2)
            nc.vector.memset(den[:, 0:2], 0.0).then_inc(small_set, 1)
            dve.wait_ge(proj_in, 48)
            for n, (dst, src, hi) in enumerate(((wqk[1][:, :, 0:D], raw_q, wqk[0][:, :, 0:D]),
                                                (wqk[1][:, :, D:2 * D], raw_k, wqk[0][:, :, D:2 * D]),
                                                (wv[1][:], raw_v, wv[0][:]),
                                                (bo_r[1][:], bo_row[:], bo_r[0][:]))):
                dve.wait_ge(hi_set, n + 1)
                minus_hi(dst, src, hi).then_inc(lo_set, 1)
            nc.vector.tensor_copy(identB[:], identF[:]).then_inc(bf_set, 1)
            nc.vector.tensor_scalar(maskB[:], upF[:], NEG, None, ALU.mult).then_inc(bf_set, 1)
            with dve.Fori(0, 6) as a:
                front_stats(a)
                front_ln(a)
                for u in FRONT_USES:
                    x_reader(*u, a, None, None)
            for k in range(NM):
                reduce_piece(0, k)
            join_maxima(0)
            x_reader("maxT", 0, None, 0, None)
            with dve.Fori(0, 2) as i:
                for par in range(2):
                    body(2 * i + par, True, True, True, False)
            with dve.Fori(2, 5) as i:
                for par in range(2):
                    body(2 * i + par, True, True, True, True)
            with dve.Fori(5, 7) as i:
                for par in range(2):
                    body(2 * i + par, True, True, False, True)
            body(14, True, True, False, True)
            body(15, True, False, False, True)
            with dve.Fori(16, 20) as t:
                body(t, False, False, False, True)

        @blk.gpsimd
        def _(pool):
            def rstd(n, s_ve, s_rs, k):
                pool.wait_ge(s_ve, k + 1)
                nc.gpsimd.tensor_tensor(rs[:, n, :], ve[:, n, :], mhalf[:], ALU.pow).then_inc(s_rs, 1)

            def place_v(t, par, quarters):
                pool.wait_ge(a_vout, LEAD + quarters)
                if not isinstance(t, int):
                    pool.wait_ge(pv_done, NS * (t - 1) + 2)
                src = v_all[:, bass.ds(8 * ((t // 4) % 2), 8), bass.ds(64 * (t % 4), 64)]\
                    .rearrange("p k (h d) -> p k h d", h=HG)
                nc.gpsimd.tensor_copy(Vg[par][:, :, :, 0:DH], src).then_inc(vg_set, 1)

            def mask(t, s):
                pool.wait_ge(exp_done, 2 * NS * t + 2 * s + 4)
                nc.gpsimd.tensor_tensor(spare_p[0:1, s + 1:s + 2], spare_p[0:1, 0:1], spare_p[0:1, 0:1], ALU.add)
                v = Pt[:, s % 2, :, 0:P]
                nc.gpsimd.affine_select(out=v, in_=v, compare_op=ALU.is_ge, fill=0.0, base=0,
                                        pattern=[[0, HG], [1, P]], channel_multiplier=-1).then_inc(p_masked, 1)

            def hidden_lo(c, j):
                pool.wait_ge(f_hi, 8 * c + j + 1)
                pool.wait_ge(c_down, LEAD + c)
                nc.gpsimd.tensor_tensor(hh[1][:, j, :], hf[:, j % 2, :], hh[0][:, j, :].bitcast(F32), ALU.subtract)\
                  .then_inc(f_lo, 1)

            def body(t, par, second, maxima, front, back):
                c = t - 4
                for s in range(NS):
                    if second and diagonal(s):
                        mask(t, s)
                    if front and s == 1:
                        rstd(0, a_ve, a_rs, t + 6)
                    if back and s == 2:
                        rstd(1, c_ve, c_rs, 3 * c)
                        pool.wait_ge(c_an, c + 1)
                        pool.wait_ge(xc_in, 16 * (c + 1))
                        nc.gpsimd.tensor_tensor(x1, an, xc, ALU.add).then_inc(c_x1, 1)
                    if back and s == 3:
                        rstd(2, c_ve, c_rs, 3 * c + 1)
                    if maxima and s == 4:
                        place_v(t + 1, (par + 1) % 2, t + 5 if front else NQ)
                    if back:
                        for j in {6: (0,), 7: (1,), 8: (2, 3), 9: (4, 5), 10: (6, 7)}.get(s, ()):
                            hidden_lo(c, j)
                    if back and s == 11:
                        rstd(3, c_ve, c_rs, 3 * c + 2)
                        pool.wait_ge(c_yn, LEAD + c + 1)
                        pool.wait_ge(y_out, LEAD + 16 * c)
                        nc.gpsimd.tensor_tensor(yo, an, x1, ALU.add).then_inc(c_y, 1)

            nc.gpsimd.memset(spare_p[:], 0.0).then_inc(spare_set, 1)
            pool.wait_ge(spare_set, 1)
            pool.wait_ge(small_set, 1)
            with pool.Fori(0, 6) as a:
                rstd(0, a_ve, a_rs, a)
            place_v(0, 0, 4)
            pool.wait_ge(had_out, 1)
            for n, (src, dst) in enumerate(((had_a, had_b), (had_b, had_a), (had_a, had_b))):
                if n:
                    pool.wait_ge(fly, 4 * n)
                for q in range(4):
                    c = (q >> n << (n + 1)) + q % 2 ** n
                    o = c + 2 ** n
                    nc.gpsimd.tensor_tensor(dst[:, c, :], src[:, c, :], src[:, o, :], ALU.add)
                    nc.gpsimd.tensor_tensor(dst[:, o, :], src[:, c, :], src[:, o, :], ALU.subtract).then_inc(fly, 1)
            pool.wait_ge(w2_hi, 1)
            nc.gpsimd.tensor_tensor(w2[1][:], had_b, w2[0][:].bitcast(F32), ALU.subtract).then_inc(w2_set, 1)
            with pool.Fori(0, 2) as i:
                for par in range(2):
                    body(2 * i + par, par, True, True, True, False)
            pool.wait_ge(w13_hi, 1)
            nc.gpsimd.tensor_tensor(w13[1][:].rearrange("p m k n -> p (m k n)"), flat,
                                    w13[0][:].rearrange("p m k n -> p (m k n)").bitcast(F32), ALU.subtract)\
              .then_inc(w13_set, 1)
            with pool.Fori(2, 5) as i:
                for par in range(2):
                    body(2 * i + par, par, True, True, True, True)
            with pool.Fori(5, 7) as i:
                for par in range(2):
                    body(2 * i + par, par, True, True, False, True)
            body(14, 0, True, True, False, True)
            body(15, 1, True, False, False, True)
            with pool.Fori(16, 20) as t:
                body(t, 0, False, False, False, True)


def kernel(**inputs):
    import numpy as np
    import concourse.bacc as bacc
    from concourse.bass_utils import run_bass_kernel_spmd

    n = np.arange(P)
    had = np.ones((1, 1), np.float32)
    while had.shape[0] < P:
        had = np.block([[had, had], [had, -had]])
    arrays = {
        "x": inputs["L0_attn_x"],
        "wqT": inputs["L0_attn_Wq"].T, "wkT": inputs["L0_attn_Wk"].T, "wvT": inputs["L0_attn_Wv"].T,
        "woT": inputs["L0_attn_Wo"].T, "bo": inputs["L0_attn_bo"],
        "w1T": inputs["L0_ffn_W1"].T, "w3T": inputs["L0_ffn_W3"].T, "w2T": inputs["L0_ffn_W2"].T,
        "had": had.astype(np.float32), "ident": np.eye(P, dtype=np.float32),
        "upper": (n[None, :] > n[:, None]).astype(np.float32),
    }
    nc = bacc.Bacc("TRN2", target_bir_lowering=False, num_devices=1)
    feeds, args = {}, []
    for name, a in arrays.items():
        a = np.ascontiguousarray(a)
        feeds[f"in_{name}"] = a
        args.append(nc.dram_tensor(f"in_{name}", a.shape, mybir.dt.from_np(a.dtype), kind="ExternalInput").ap())
    out = nc.dram_tensor("out_0", (B, S, D), F32, kind="ExternalOutput").ap()
    block(nc, *args, out)
    r = run_bass_kernel_spmd(nc, [feeds], core_ids=[0])
    return r.results[0]["out_0"]
```

```python
from contextlib import ExitStack

import concourse.bass as bass
from concourse import mybir

F32 = mybir.dt.float32
F32R = mybir.dt.float32r
BF16 = mybir.dt.bfloat16
ALU = mybir.AluOpType
ACT = mybir.ActivationFunctionType
AX = mybir.AxisListType

P = 128
B, S, D, H = 4, 1024, 256, 1024
HEADS, DH = 16, 16
HG = 4
KC = D // P
QT = 256
NQ = B * S // QT
NT = B * HEADS // HG
NF = H // P
EPS = 1e-5
SCALE = 0.25
NEG = -1e30
CH = 512
LEAD = 16
MB = 3

STEPS = [(c, kb) for c in range(S // CH) for kb in range(4 * c + 4)]
PIECES = [(p, i, r) for c in range(2) for p in range(2) for i in range(4 * c, 4 * c + 4) for r in range(c + 1)]
NS, NM = len(STEPS), len(PIECES)
M_AT = [0, 3, 3, 2, 2, 2, 2, 2, 2, 2, 2, 2]
M_FROM = [sum(M_AT[:s]) for s in range(NS)]

X_AT = {
    (0, 0): ("ffn", 0), (0, 1): ("ffn", 1), (1, 0): ("maxT", 1), (1, 1): ("ffn", 2), (2, 0): ("ffn", 3),
    (2, 1): ("lnT", 0), (3, 0): ("ffn", 4), (3, 1): ("qk", 0), (4, 0): ("ffn", 5), (4, 1): ("qk", 1),
    (5, 0): ("attn", 0), (5, 1): ("maxT", 0), (6, 0): ("ffn", 6), (7, 0): ("ffn", 7),
    (8, 0): ("down", 0), (10, 0): ("ln2T", 0), (11, 0): ("v", 0),
}
HALF_AT = {("down", 0): (9, 1), ("v", 0): (11, 1)}
X_READ = {HALF_AT.get(u, at): u for at, u in X_AT.items()}
FFN_AT = {u[1]: 2 * at[0] + at[1] for at, u in X_AT.items() if u[0] == "ffn"}
LO_BEFORE = {1: (0,), 5: (4,), 6: (5,), 7: (6,), 8: (7,)}
LO_AFTER = {1: (1,), 2: (2,), 3: (3,)}
FRONT_USES = [("lnT", 0), ("qk", 0), ("qk", 1), ("v", 0)]


def uses_of(second, maxima, front, wo_stage, ffn_stage):
    has = {("maxT", 1): second, ("maxT", 0): maxima, "lnT": front, "qk": front, "v": front, "attn": wo_stage, "ln2T": wo_stage,
           "ffn": ffn_stage, "down": ffn_stage}
    order = [X_AT[k] for k in sorted(X_AT)]
    return {u: n for n, u in enumerate(u for u in order if has.get(u, has.get(u[0])))}


def diagonal(s):
    c, kb = STEPS[s]
    return kb >= 4 * c


def span(s):
    c, kb = STEPS[s]
    q0 = max(CH * c, P * kb)
    return q0, CH * (c + 1) - q0


def piece(k):
    p, i, r = PIECES[k]
    k0 = 512 * r
    w = min(512, P * (i + 1) - k0)
    return p, i, r, k0, w, k0 + w == P * (i + 1)


def each_body(eng, body):
    body(-1, 1, False, True, True, False, False)
    with eng.Fori(0, 2) as i:
        for par in range(2):
            body(2 * i + par, par, True, True, True, False, False)
    body(4, 0, True, True, True, True, False)
    with eng.Fori(2, 5) as i:
        for par in (1, 2):
            body(2 * i + par, par % 2, True, True, True, True, True)
    with eng.Fori(5, 7) as i:
        for par in (1, 2):
            body(2 * i + par, par % 2, True, True, False, True, True)
    body(15, 1, True, False, False, True, True)
    with eng.Fori(8, 10) as i:
        for par in range(2):
            body(2 * i + par, par, False, False, False, True, True)
    body(20, 0, False, False, False, False, True)


def block(nc, x, wqT, wkT, wvT, woT, bo, w1T, w3T, w2T, had, ident, upper, out):
    ctx = ExitStack()
    with ctx:
        def sb(name, shape, dt=F32):
            return ctx.enter_context(nc.sbuf_tensor(name, shape, dt))

        def sem(name):
            return ctx.enter_context(nc.semaphore(name))

        qk_dram = nc.dram_tensor("qk_scratch", [B, 4, 3, P, S], F32).ap()
        o_dram = nc.dram_tensor("o_scratch", [B, 2, HEADS, 32, CH], F32).ap()
        r_dram = nc.dram_tensor("r_scratch", [NQ, HEADS, QT], F32).ap()

        identF = sb("identF", [P, P])
        hadF = sb("hadF", [P, P])
        upF = sb("upF", [P, P])
        identB = sb("identB", [P, P], BF16)
        maskB = sb("maskB", [P, P], BF16)
        mhalf = sb("mhalf", [P, 2])
        spare = sb("spare", [P, 2])
        spare_p = sb("spare_p", [P, NS + 1])
        wqk = [sb(f"wqk_{n}", [P, KC, 2 * D], F32R) for n in ("hi", "lo")]
        wv = [sb(f"wv_{n}", [P, KC, D], F32R) for n in ("hi", "lo")]
        wo = sb("wo", [P, KC, D])
        bo_row = sb("bo_row", [1, D])
        bo_r = [sb(f"bo_{n}", [1, D], F32R) for n in ("hi", "lo")]
        ones = sb("ones", [1, P], F32R)
        w13 = [sb(f"w13_{n}", [P, 2, KC, H], F32R) for n in ("hi", "lo")]
        w2 = [sb(f"w2_{n}", [P, NF, D], F32R) for n in ("hi", "lo")]
        xa = sb("xa", [P, 2, D])
        xn = sb("xn", [P, 2, D])
        xT = [sb(f"xT_{n}", [P, KC, QT], F32R) for n in ("hi", "lo")]
        qk = [sb(f"qk_{n}", [P, 4, QT], F32R) for n in ("hi", "lo")]
        v_all = sb("v_all", [P, 2 * S // P, D])
        Qs = [sb(f"Qs{i}", [P, 2, S], F32R) for i in range(2)]
        Ks = [sb(f"Ks{i}", [P, 2, S], F32R) for i in range(2)]
        Vg = [sb(f"Vg{i}", [P, S // P, HG, 32]) for i in range(2)]
        Pt = sb("Pt", [P, 2, HG, CH])
        m0 = sb("m0", [P, HG, 8])
        m1 = sb("m1", [P, HG, 4])
        mcat = sb("mcat", [P, 2, HG, 2, 4], F32R)
        mrow = sb("mrow", [32, 2, P], F32R)
        On = sb("On", [P, 2, CH])
        work = sb("work", [P, 8, 512])
        xc, oc, an, xn2, yr, yo, th, hf = (work[:, i, :].rearrange("p (j d) -> p j d", j=2) for i in range(8))
        x1 = [sb(f"x1_{i}", [P, 2, D])[:] for i in range(2)]
        rb = sb("rb", [P, KC, QT])
        dn = sb("dn", [P, 32])
        dr = sb("dr", [P, 32])
        hw = sb("hw", [P, 2, QT])
        nT = [sb(f"nT_{n}", [P, KC, QT], F32R) for n in ("hi", "lo")]
        hh = [sb(f"hh_{n}", [P, NF, QT], F32R) for n in ("hi", "lo")]
        st6 = sb("st6", [P, 4, 2, 6])
        mv = sb("mv", [P, 4, 2, 2])
        ve = sb("ve", [P, 4, 2])
        rs = sb("rs", [P, 4, 2])
        nmr = sb("nmr", [P, 4, 2])
        raw = Pt[:].rearrange("p a h q -> p (a h q)")
        flat = work[:].rearrange("p a q -> p (a q)")
        raw_q, raw_k, raw_v = (raw[:, i * 512:(i + 1) * 512].rearrange("p (k n) -> p k n", k=KC) for i in range(3))
        raw_w2 = raw[:, 2048:4096].rearrange("p (c n) -> p c n", c=NF)
        had_a = flat[:, 0:2048].rearrange("p (c n) -> p c n", c=NF)
        had_b = flat[:, 2048:4096].rearrange("p (c n) -> p c n", c=NF)
        raw_w13 = flat.rearrange("p (m k n) -> p m k n", m=2, k=KC)

        def w13_part(half, t):
            return w13[half][:].rearrange("p m k n -> p (m k n)")[:, bass.ds(1024 * t, 1024)]

        Sp = ctx.enter_context(nc.psum_tensor("Sp", [P, 2, 512], F32))
        Mp = ctx.enter_context(nc.psum_tensor("Mp", [P, MB, 512], F32))
        Vp = ctx.enter_context(nc.psum_tensor("Vp", [P, 512], F32))
        Xp = ctx.enter_context(nc.psum_tensor("Xp", [P, 2, 512], F32))

        def X2(bank):
            return Xp[:, bank, :].rearrange("p (j d) -> p j d", j=2)

        consts_in = sem("consts_in")
        proj_in = sem("proj_in")
        w2_in = sem("w2_in")
        w13_in = sem("w13_in")
        small_set = sem("small_set")
        spare_set = sem("spare_set")
        bf_set = sem("bf_set")
        hi_set = sem("hi_set")
        lo_set = sem("lo_set")
        had_done = sem("had_done")
        had_out = sem("had_out")
        fly = sem("fly")
        w2_hi = sem("w2_hi")
        w2_set = sem("w2_set")
        w13_hi = sem("w13_hi")
        w13_set = sem("w13_set")
        xa_in = sem("xa_in")
        a_st, a_mv, a_ve, a_rs, a_xn = (sem(n) for n in ("a_st", "a_mv", "a_ve", "a_rs", "a_xn"))
        a_T, a_hi, a_lo = sem("a_T"), sem("a_hi"), sem("a_lo")
        a_qk, a_qkhi, a_qklo = sem("a_qk"), sem("a_qkhi"), sem("a_qklo")
        qk_out = sem("qk_out")
        a_v, a_vout = sem("a_v"), sem("a_vout")
        stacked = [sem(f"stacked{p}") for p in range(2)]
        vg_set = sem("vg_set")
        m_full, m_red = sem("m_full"), sem("m_red")
        m_all, m_hi, m_cat, m_T, m_row = (sem(n) for n in ("m_all", "m_hi", "m_cat", "m_T", "m_row"))
        mrow_in = [sem(f"mrow_in{c}") for c in range(2)]
        s_full, exp_done = sem("s_full"), sem("exp_done")
        p_masked = sem("p_masked")
        pv_done = sem("pv_done")
        o_copy = sem("o_copy")
        o_out = [sem(f"o_out{c}") for c in range(2)]
        dn_in, rd_out, rb_in, xc_in, oc_in = (sem(n) for n in ("dn_in", "rd_out", "rb_in", "xc_in", "oc_in"))
        c_dr, c_on, c_attn, c_raw, c_an, c_x1, c_xn2 = (
            sem(n) for n in ("c_dr", "c_on", "c_attn", "c_raw", "c_an", "c_x1", "c_xn2"))
        c_st, c_mv, c_ve, c_rs = (sem(n) for n in ("c_st", "c_mv", "c_ve", "c_rs"))
        c_nmr, c_T, c_hi, c_lo = (sem(n) for n in ("c_nmr", "c_T", "c_hi", "c_lo"))
        f_gu, f_th, f_w, f_h, f_hi, f_lo = (sem(n) for n in ("f_gu", "f_th", "f_w", "f_h", "f_hi", "f_lo"))
        f_down, f_raw, f_st, f_mv, f_ve, f_rs, f_nmr, f_yn, f_y, y_out = (
            sem(n) for n in ("f_down", "f_raw", "f_st", "f_mv", "f_ve", "f_rs", "f_nmr", "f_yn", "f_y", "y_out"))
        led = (a_qkhi, a_qklo, s_full, exp_done, pv_done, m_red, a_xn, a_v, a_vout, a_T, qk_out, vg_set, m_row, m_T, *mrow_in, o_copy,
               *o_out, rb_in, c_dr, c_on, c_attn, c_raw, c_x1, c_T, c_lo, f_gu, f_lo, f_down, f_raw, f_y, y_out)

        def after(s, n):
            return n + LEAD if any(s is l for l in led) else n

        x_rows = x.rearrange("b (q j p) d -> (b q) p j d", j=2, p=P)
        out_rows = out.rearrange("b (q j p) d -> (b q) p j d", j=2, p=P)

        blk = ctx.enter_context(nc.Block())

        @blk.sync
        def _(sp):
            def load_xa(a):
                sp.wait_ge(a_xn, after(a_xn, a))
                sp.dma_start(xa[:], x_rows[a % NQ]).then_inc(xa_in, 16)

            def store_qk(a):
                sp.wait_ge(a_qkhi, after(a_qkhi, 2 * a + 2))
                sp.wait_ge(a_qklo, after(a_qklo, 2 * a + 2))
                cols = bass.ds((a % 4) * QT, QT)
                for half, m0_, m1_, slot in ((0, 0, 4, 0), (1, 0, 2, 1), (0, 0, 2, 2), (0, 2, 4, 1), (1, 2, 4, 2)):
                    sp.dma_start(qk_dram[a // 4, m0_:m1_, slot, :, cols].rearrange("m p t -> p m t"),
                                 qk[half][:, m0_:m1_, :].bitcast(F32)).then_inc(qk_out, 16)

            def stack(t, par, p):
                if isinstance(t, int) and t < 2:
                    sp.wait_ge(small_set, 1)
                elif p == 0:
                    sp.wait_ge(s_full, after(s_full, 2 * NS * (t - 1)))
                g = t % 4
                for dst, kind in ((Qs, 0), (Ks, 2)):
                    for half in range(2):
                        rows = bass.ds((g % 2) * 64 + (2 * p + half) * DH, DH)
                        sp.dma_start(dst[par][64 * half:64 * half + 48, p, :].bitcast(F32),
                                     qk_dram[(t // 4) % B, kind + g // 2, :, rows, :]).then_inc(stacked[p], 16)

            def maxima_rows(t, par, c, front=False):
                sp.wait_ge(m_row, after(m_row, 2 * t + c + 1))
                for h in range(HG):
                    row = 64 * (h % 2) + 48
                    if front and h == HG - 1:
                        sp.wait_ge(qk_out, after(qk_out, 80 * (t + 5)))
                    sp.dma_start(Qs[par][row:row + 2, h // 2, c * CH:(c + 1) * CH].bitcast(F32),
                                 mrow[8 * h:8 * h + 8, c, :].bitcast(F32)).then_inc(mrow_in[c], 16)

            def store_o(t, c):
                sp.wait_ge(o_copy, after(o_copy, 2 * t + c + 1))
                sp.dma_start(o_dram[t // 4, c, bass.ds((t % 4) * HG, HG)].rearrange("h r q -> (h r) q"),
                             On[:, c, :]).then_inc(o_out[c], 16)

            def load_denominators(c, units):
                sp.wait_ge(c_dr, after(c_dr, c))
                for o in o_out:
                    sp.wait_ge(o, after(o, 16 * units))
                q = c % 4
                sp.dma_start(dn[:], o_dram[c // 4, q // 2, :, DH, bass.ds((q % 2) * QT, QT)]
                             .rearrange("h (a b) -> h a b", b=32)).then_inc(dn_in, 16)

            def load_o(c, par):
                sp.wait_ge(c_attn, after(c_attn, c))
                sp.wait_ge(c_x1, after(c_x1, c))
                sp.dma_start(xc, x_rows[c]).then_inc(xc_in, 16)
                q = c % 4
                for k in range(KC):
                    sp.dma_start(oc[:, k, :], o_dram[c // 4, q // 2, 8 * k:8 * k + 8, 0:DH,
                                                     bass.ds((q % 2) * QT, QT)]).then_inc(oc_in, 16)

            def spread_reciprocals(c):
                sp.wait_ge(c_dr, after(c_dr, c + 1))
                sp.dma_start(r_dram[c].rearrange("h (a b) -> (h a) b", b=32), dr[:]).then_inc(rd_out, 16)
                sp.wait_ge(c_on, after(c_on, c))
                sp.wait_ge(rd_out, 16 * (c + 1))
                for k in range(KC):
                    sp.dma_start(rb[:, k, :], r_dram[c, 8 * k:8 * k + 8].rearrange("h (o t) -> h o t", o=1)
                                 .to_broadcast([8, DH, QT])).then_inc(rb_in, 16)

            def store_y(c):
                sp.wait_ge(f_y, after(f_y, c + 1))
                sp.dma_start(out_rows[c], yo).then_inc(y_out, 16)

            def body(t, par, second, maxima, front, wo_stage, ffn_stage):
                if isinstance(t, int) and t == -1:
                    sp.wait_ge(qk_out, after(qk_out, 80 * 4))
                    for p in range(2):
                        stack(0, 0, p)
                if isinstance(t, int) and t == 4:
                    sp.wait_ge(w13_set, 4)
                if wo_stage:
                    load_denominators(t - 4, t if second else NT)
                if second:
                    maxima_rows(t, par, 1)
                if front:
                    load_xa(t + 6)
                if wo_stage:
                    load_o(t - 4, par)
                    spread_reciprocals(t - 4)
                if front:
                    store_qk(t + 5)
                if second:
                    store_o(t, 0)
                if maxima:
                    maxima_rows(t + 1, (par + 1) % 2, 0, front)
                if maxima:
                    stack(t + 2, par, 0)
                if second:
                    store_o(t, 1)
                if maxima:
                    stack(t + 2, par, 1)
                if ffn_stage:
                    store_y(t - 5)

            for s in led:
                sp.sem_inc(s, LEAD)
            sp.dma_start(xa[:], x_rows[0]).then_inc(xa_in, 16)
            for dst, src in ((raw_q, wqT), (raw_k, wkT), (raw_v, wvT)):
                sp.dma_start(dst, src.rearrange("(k p) n -> p k n", p=P)).then_inc(proj_in, 16)
            for dst, src in ((identF[:], ident), (hadF[:], had), (upF[:], upper),
                             (wo[:], woT.rearrange("(k p) n -> p k n", p=P)),
                             (bo_row[:], bo.rearrange("(o n) -> o n", o=1))):
                sp.dma_start(dst, src).then_inc(consts_in, 16)
            sp.dma_start(raw_w2, w2T.rearrange("(c p) n -> p c n", p=P)).then_inc(w2_in, 16)
            with sp.Fori(0, 4) as a:
                load_xa(a + 1)
                store_qk(a)

            def bodies(t, *rest):
                body(t, *rest)
                if isinstance(t, int) and t == -1:
                    sp.wait_ge(w2_set, 1)
                    for m, src in enumerate((w1T, w3T)):
                        sp.dma_start(raw_w13[:, m], src.rearrange("(k p) n -> p k n", p=P)).then_inc(w13_in, 16)

            each_body(sp, bodies)
            sp.wait_ge(y_out, after(y_out, 16 * NQ))
            sp.wait_ge(xa_in, 16 * (NQ + 1))
            for s in stacked:
                sp.wait_ge(s, 64 * (NT + 1))
            sp.wait_ge(qk_out, after(qk_out, 80 * NQ))
            sp.wait_ge(rd_out, 16 * NQ)
            for o in o_out:
                sp.wait_ge(o, after(o, 16 * NT))

        @blk.tensor
        def _(pe):
            def split_products(dst, left, right, lcols, rcols, k_chunks):
                n = 0
                for lh, rh in ((0, 0), (0, 1), (1, 0)):
                    for k in range(k_chunks):
                        mm = nc.tensor.matmul(dst, left[lh][:, k, lcols], right[rh][:, k, rcols],
                                              start=(n == 0), stop=(n == 3 * k_chunks - 1))
                        n += 1
                return mm

            def x_read(kind, j, a, t, c, f):
                s, n = {"lnT": lambda: (a_lo, a + 1), "qk": lambda: (a_qklo, 2 * a + j + 1),
                        "v": lambda: (a_vout, a + 1), "maxT": lambda: (m_row, 2 * (t - j) + j + 1),
                        "attn": lambda: (c_raw, c + 1), "ln2T": lambda: (c_lo, c + 1),
                        "ffn": lambda: (f_h, 8 * f + j + 1), "down": lambda: (f_raw, f + 1)}[kind]()
                pe.wait_ge(s, after(s, n))

            def x_part(kind, j, bank, i, a, t, c, f):
                half = Xp[:, bank, i * QT:(i + 1) * QT]
                if kind == "lnT":
                    if i == 0:
                        pe.wait_ge(a_xn, after(a_xn, a + 1))
                    for k in range(2):
                        mm = nc.tensor.transpose(half[:, k * P:(k + 1) * P], xn[:, k, i * P:(i + 1) * P], identF[:])
                    done = a_T
                elif kind == "qk":
                    if i == 0:
                        pe.wait_ge(a_hi, a + 1)
                        pe.wait_ge(a_lo, a + 1)
                    m = 2 * j + i
                    mm = split_products(half, wqk, xT, slice(m * P, (m + 1) * P), slice(0, QT), KC)
                    done = a_qk
                elif kind == "v":
                    mm = split_products(half, xT, wv, slice(i * P, (i + 1) * P), slice(0, D), KC)
                    done = a_v
                elif kind == "maxT":
                    if i == 1:
                        return
                    pe.wait_ge(m_cat, 2 * (t - j) + j + 1)
                    nc.tensor.matmul(Xp[0:32, bank, 0:P], mcat[:, j].rearrange("p h n i -> p (h n i)").bitcast(F32),
                                     identF[:], start=True, stop=True).then_inc(m_T, 1)
                    return
                elif kind == "attn":
                    if i == 0:
                        pe.wait_ge(c_on, after(c_on, c + 1))
                    for k in range(KC):
                        nc.tensor.matmul(half, oc[:, k, i * P:(i + 1) * P], wo[:, k, :], start=(k == 0), stop=False)
                    for n in range(2):
                        mm = nc.tensor.matmul(half, ones[0:1, :], bo_r[n][0:1, :], start=False, stop=(n == 1))
                    done = c_attn
                elif kind == "ln2T":
                    if i == 0:
                        pe.wait_ge(c_xn2, c + 1)
                    for k in range(2):
                        mm = nc.tensor.transpose(half[:, k * P:(k + 1) * P], xn2[:, k, i * P:(i + 1) * P], identF[:])
                    done = c_T
                elif kind == "ffn":
                    if j == 0 and i == 0:
                        pe.wait_ge(c_hi, f + 1)
                        pe.wait_ge(c_lo, after(c_lo, f + 1))
                    mm = split_products(half, [w13[h][:, i] for h in range(2)], nT, slice(j * P, (j + 1) * P),
                                        slice(0, QT), KC)
                    done = f_gu
                elif kind == "down":
                    for k in range(NF):
                        if i == 0 and k in (0, NF - 1):
                            pe.wait_ge(f_lo, after(f_lo, 8 * f + (NF if k else NF - 1)))
                        for n, (lh, rh) in enumerate(((0, 0), (0, 1), (1, 0))):
                            mm = nc.tensor.matmul(half, hh[lh][:, k, i * P:(i + 1) * P], w2[rh][:, k, :],
                                                  start=(k == 0 and n == 0), stop=(k == NF - 1 and n == 2))
                    done = f_down
                if i == 1:
                    mm.then_inc(done, 1)

            def max_piece(t, par, k):
                p, i, r, k0, w, diag = piece(k)
                if k in (0, 4):
                    pe.wait_ge(stacked[p], 64 * (t + 1))
                for half in range(2):
                    lo, n = 64 * half, 2 * k + half
                    if not (isinstance(t, int) and t == 0 and n < MB):
                        pe.wait_ge(m_red, after(m_red, 2 * NM * t + n - MB + 1))
                    mm = nc.tensor.matmul(Mp[:, n % MB, 0:w], Qs[par][lo:lo + 48, p, i * P:(i + 1) * P],
                                          Ks[par][lo:lo + 48, p, k0:k0 + w], start=True, stop=not diag)
                    if not diag:
                        mm.then_inc(m_full, 1)
                if diag:
                    for half in range(2):
                        nc.tensor.matmul(Mp[:, (2 * k + half) % MB, w - P:w], identB[:], maskB[:],
                                         start=False, stop=True).then_inc(m_full, 1)

            def scores(t, par, s, p):
                c, kb = STEPS[s]
                q0, n = span(s)
                if kb == 0 and p == 0:
                    pe.wait_ge(mrow_in[c], after(mrow_in[c], 64 * (t + 1)))
                pe.wait_ge(exp_done, after(exp_done, 2 * NS * t + 2 * s + p))
                for half in range(2):
                    lo = 64 * half
                    mm = nc.tensor.matmul(Sp[:, half, 0:n], Ks[par][lo:lo + 50, p, kb * P:(kb + 1) * P],
                                          Qs[par][lo:lo + 50, p, q0:q0 + n], start=True, stop=True)
                mm.then_inc(s_full, 1)

            def pv(t, par, s):
                c, kb = STEPS[s]
                q0, n = span(s)
                if s == 0:
                    pe.wait_ge(vg_set, after(vg_set, t + 1))
                if kb == 0:
                    pe.wait_ge(o_copy, after(o_copy, 2 * t + c))
                if diagonal(s):
                    pe.wait_ge(p_masked, 8 * t + kb + 1)
                else:
                    pe.wait_ge(exp_done, after(exp_done, 2 * NS * t + 2 * s + 2))
                for h in range(HG):
                    mm = nc.tensor.matmul(Vp[32 * h:32 * h + 32, CH - n:CH], Vg[par][:, kb, h, :],
                                          Pt[:, s % 2, h, 0:n], start=(kb == 0), stop=(kb == 4 * c + 3))
                mm.then_inc(pv_done, 1)

            def first_uses(t, second, maxima, front, wo_stage, ffn_stage):
                if second:
                    pe.wait_ge(m_row, after(m_row, 2 * t + 1))
                pe.wait_ge(a_vout, after(a_vout, t + 5 if front else NQ))
                if front:
                    pe.wait_ge(a_qklo, after(a_qklo, 2 * (t + 5)))
                if wo_stage or ffn_stage:
                    pe.wait_ge(c_lo, after(c_lo, t - 4))
                if ffn_stage:
                    pe.wait_ge(f_raw, after(f_raw, t - 5))

            def body(t, par, second, maxima, front, wo_stage, ffn_stage):
                numbers = uses_of(second, maxima, front, wo_stage, ffn_stage)
                order = list(numbers)
                counts = (t + 5, t + 1, t - 4, t - 5)
                first_uses(t, second, maxima, front, wo_stage, ffn_stage)

                def use_half(s, place, i):
                    for at, u in X_AT.items():
                        if u not in numbers or (s, place) != (HALF_AT.get(u, at) if i else at):
                            continue
                        n = numbers[u]
                        if i == 0 and n >= 2:
                            x_read(*order[n - 2], *counts)
                        x_part(*u, n % 2, i, *counts)

                for s in range(NS):
                    m = list(range(M_FROM[s], M_FROM[s] + M_AT[s])) if maxima else []
                    for place in range(2):
                        if len(m) > place:
                            max_piece(t + 1, (par + 1) % 2, m[place])
                        if second:
                            scores(t, par, s, place)
                        use_half(s, place, 0)
                        if place == 1 and len(m) > 2:
                            max_piece(t + 1, (par + 1) % 2, m[2])
                        use_half(s, place, 1)
                    if second and s:
                        pv(t, par, s - 1)
                if second:
                    pv(t, par, NS - 1)

            pe.wait_ge(consts_in, 16 * 5)
            pe.wait_ge(hi_set, 4)
            pe.wait_ge(lo_set, 4)
            pe.wait_ge(small_set, 1)
            with pe.Fori(0, 4) as a:
                for n, u in enumerate(FRONT_USES):
                    if n >= 2:
                        x_read(*FRONT_USES[n - 2], a, None, None, None)
                    else:
                        pe.wait_ge(a_vout, after(a_vout, a))
                        pe.wait_ge(a_qklo, after(a_qklo, 2 * a))
                    for i in range(2):
                        x_part(*u, n % 2, i, a, None, None, None)
            pe.wait_ge(bf_set, 2)
            pe.wait_ge(w2_in, 16)

            for c in range(NF):
                if c == NF // 2:
                    pe.wait_ge(had_out, 1)
                mm = nc.tensor.matmul(Sp[:, c // 2 % 2, (c % 2) * D:(c % 2 + 1) * D], hadF[:], raw_w2[:, c, :],
                                      start=True, stop=True)
                if c % 4 == 3:
                    mm.then_inc(had_done, 1)
            pe.wait_ge(had_out, 2)

            def bodies(t, *rest):
                if isinstance(t, int) and t == 4:
                    pe.wait_ge(w2_set, 1)
                    pe.wait_ge(w13_set, 4)
                body(t, *rest)

            each_body(pe, bodies)

        @blk.scalar
        def _(act):
            def copy(dst, src, **kw):
                return nc.scalar.activation(dst, src, ACT.Copy, **kw)

            def x_reader(kind, j, bank, a, t, c, f, reused=True):
                whole = Xp[:, bank, :]
                if kind == "lnT":
                    act.wait_ge(a_T, after(a_T, a + 1))
                    act.wait_ge(a_v, after(a_v, a))
                    copy(xT[0][:].rearrange("p k t -> p (k t)"), whole).then_inc(a_hi, 1)
                elif kind == "qk":
                    act.wait_ge(a_qk, 2 * a + j + 1)
                    if j == 0:
                        act.wait_ge(qk_out, after(qk_out, 80 * a))
                    copy(qk[0][:, 2 * j:2 * j + 2, :], X2(bank)).then_inc(a_qkhi, 1)
                elif kind == "v":
                    act.wait_ge(a_v, after(a_v, a + 1))
                    if reused:
                        act.wait_ge(vg_set, after(vg_set, a - 4))
                    copy(v_all[:, bass.ds(2 * (a % 8), 2), :], X2(bank)).then_inc(a_vout, 1)
                elif kind == "maxT":
                    u = t - j
                    act.wait_ge(m_T, after(m_T, 2 * u + j + 1))
                    act.wait_ge(mrow_in[j], after(mrow_in[j], 64 * u))
                    copy(mrow[:, j, :], Xp[0:32, bank, 0:P]).then_inc(m_row, 1)
                elif kind == "attn":
                    act.wait_ge(c_attn, after(c_attn, c + 1))
                    act.wait_ge(c_x1, after(c_x1, c))
                    copy(an, X2(bank)).then_inc(c_raw, 1)
                elif kind == "ln2T":
                    act.wait_ge(c_T, after(c_T, c + 1))
                    act.wait_ge(f_gu, after(f_gu, 8 * c))
                    copy(nT[0][:].rearrange("p k t -> p (k t)"), whole).then_inc(c_hi, 1)
                elif kind == "ffn":
                    act.wait_ge(f_gu, after(f_gu, 8 * f + j + 1))
                    nc.scalar.activation(th[:, j % 2, :], Xp[:, bank, 0:QT], ACT.Tanh, scale=0.5).then_inc(f_th, 1)
                elif kind == "down":
                    act.wait_ge(f_down, after(f_down, f + 1))
                    act.wait_ge(f_y, after(f_y, f))
                    copy(yr, X2(bank)).then_inc(f_raw, 1)

            def hidden_hi(f, j):
                act.wait_ge(f_h, 8 * f + j + 1)
                if j == 0:
                    act.wait_ge(f_down, after(f_down, f))
                copy(hh[0][:, j, :], hf[:, j % 2, :]).then_inc(f_hi, 1)

            def normalise(n, tile, count, s_nmr, done):
                act.wait_ge(s_nmr, count + 1)
                for i in range(2):
                    last = nc.scalar.activation(tile[:, i, :], tile[:, i, :], ACT.Identity, bias=nmr[:, n, i:i + 1],
                                                scale=rs[:, n, i:i + 1])
                last.then_inc(done, 1)

            def exps(t, s, p):
                _, n = span(s)
                act.wait_ge(s_full, after(s_full, 2 * NS * t + 2 * s + p + 1))
                if p == 0:
                    act.wait_ge(pv_done, after(pv_done, NS * t + s - 1))
                nc.scalar.activation(Pt[:, s % 2, 2 * p:2 * p + 2, 0:n], Sp[:, :, 0:n], ACT.Exp,
                                     scale=SCALE).then_inc(exp_done, 1)

            def copy_o(t, c):
                act.wait_ge(pv_done, after(pv_done, NS * t + 4 + 8 * c))
                act.wait_ge(o_out[c], after(o_out[c], 16 * t))
                copy(On[:, c, :], Vp[:, :]).then_inc(o_copy, 1)

            def body(t, par, second, maxima, front, wo_stage, ffn_stage):
                numbers = uses_of(second, maxima, front, wo_stage, ffn_stage)
                for s in range(NS):
                    for place in range(2):
                        if ffn_stage:
                            for j, at in FFN_AT.items():
                                if 2 * s + place == at + 2:
                                    hidden_hi(t - 5, j)
                        if second:
                            exps(t, s, place)
                        if wo_stage and (s, place) == (7, 0):
                            normalise(1, an, t - 4, c_nmr, c_an)
                        if second and s == 5 and place == 0:
                            copy_o(t, 0)
                        u = X_READ.get((s, place))
                        if u in numbers:
                            x_reader(*u, numbers[u] % 2, t + 5, t + 1, t - 4, t - 5)
                    if isinstance(t, int) and t == -1 and s == 8:
                        act.wait_ge(fly, 12)
                        copy(w2[0][:], had_b).then_inc(w2_hi, 1)
                    if second and front and not wo_stage and s == 8:
                        act.wait_ge(w13_in, 32)
                        copy(w13_part(0, t), flat[:, bass.ds(1024 * t, 1024)]).then_inc(w13_hi, 1)
                if second:
                    copy_o(t, 1)
                if ffn_stage:
                    normalise(3, yr, t - 5, f_nmr, f_yn)

            act.wait_ge(proj_in, 48)
            copy(wqk[0][:, :, 0:D], raw_q).then_inc(hi_set, 1)
            copy(wqk[0][:, :, D:2 * D], raw_k).then_inc(hi_set, 1)
            copy(wv[0][:], raw_v).then_inc(hi_set, 1)
            act.wait_ge(consts_in, 16 * 5)
            copy(bo_r[0][:], bo_row[:]).then_inc(hi_set, 1)
            with act.Fori(0, 4) as a:
                for n, u in enumerate(FRONT_USES):
                    x_reader(*u, n % 2, a, None, None, None, reused=False)

            for n in range(2):
                act.wait_ge(had_done, n + 1)
                copy(flat[:, n * 1024:(n + 1) * 1024], Sp[:].rearrange("p b n -> p (b n)"),
                     scale=1.0 / 64).then_inc(had_out, 1)
            each_body(act, body)

        @blk.vector
        def _(dve):
            def minus_hi(dst, src, hi):
                return nc.vector.tensor_tensor(dst, src, hi.bitcast(F32), ALU.subtract)

            def stats(n, src, k, s_st, s_mv, s_ve):
                for i in range(2):
                    last = nc.vector.bn_stats(st6[:, n, i, :], src[:, i, :])
                last.then_inc(s_st, 1)
                dve.wait_ge(s_st, k + 1)
                nc.vector.memset(spare[0:1, 0:1], 0.0)
                for i in range(2):
                    last = nc.vector.bn_aggr(mv[:, n, i, :], st6[:, n, i, :])
                last.then_inc(s_mv, 1)
                dve.wait_ge(s_mv, k + 1)
                nc.vector.tensor_scalar(ve[:, n, :], mv[:, n, :, 1], EPS, None, ALU.add).then_inc(s_ve, 1)

            def apply_ln(n, dst, src, done):
                for i in range(2):
                    last = nc.vector.tensor_scalar(dst[:, i, :], src[:, i, :], mv[:, n, i, 0:1], rs[:, n, i:i + 1],
                                                   ALU.subtract, ALU.mult)
                last.then_inc(done, 1)

            def front_stats(a):
                dve.wait_ge(xa_in, 16 * (a + 1))
                stats(0, xa, a, a_st, a_mv, a_ve)

            def front_ln(a):
                dve.wait_ge(a_rs, a + 1)
                dve.wait_ge(a_T, after(a_T, a))
                apply_ln(0, xn, xa, a_xn)

            def shift(n, s_rs, k, done):
                dve.wait_ge(s_rs, k)
                nc.vector.scalar_tensor_tensor(nmr[:, n, :], mv[:, n, :, 0], -1.0, rs[:, n, :], ALU.mult, ALU.mult)\
                  .then_inc(done, 1)

            def reciprocals(c):
                dve.wait_ge(dn_in, 16 * (c + 1))
                nc.vector.reciprocal(dr[:], dn[:]).then_inc(c_dr, 1)

            def normalise_o(c):
                dve.wait_ge(rb_in, after(rb_in, 32 * (c + 1)))
                dve.wait_ge(oc_in, 32 * (c + 1))
                nc.vector.tensor_tensor(oc, oc, rb[:], ALU.mult).then_inc(c_on, 1)

            def x_reader(kind, j, bank, a, t, c, f):
                whole = Xp[:, bank, :]
                if kind == "lnT":
                    dve.wait_ge(a_hi, a + 1)
                    minus_hi(xT[1][:].rearrange("p k t -> p (k t)"), whole, xT[0][:].rearrange("p k t -> p (k t)"))\
                        .then_inc(a_lo, 1)
                elif kind == "qk":
                    dve.wait_ge(a_qkhi, after(a_qkhi, 2 * a + j + 1))
                    minus_hi(qk[1][:, 2 * j:2 * j + 2, :], X2(bank), qk[0][:, 2 * j:2 * j + 2, :])\
                        .then_inc(a_qklo, 1)
                elif kind == "ln2T":
                    dve.wait_ge(c_hi, c + 1)
                    minus_hi(nT[1][:].rearrange("p k t -> p (k t)"), whole, nT[0][:].rearrange("p k t -> p (k t)"))\
                        .then_inc(c_lo, 1)
                elif kind == "ffn":
                    dve.wait_ge(f_th, 8 * f + j + 1)
                    nc.vector.scalar_tensor_tensor(hw[:, j % 2, :], th[:, j % 2, :], 1.0, Xp[:, bank, 0:QT], ALU.add, ALU.mult)\
                      .then_inc(f_w, 1)
                    dve.wait_ge(f_w, 8 * f + j + 1)
                    dve.wait_ge(f_lo, after(f_lo, 8 * f + j - 1 if j >= 2 else 8 * f))
                    nc.vector.tensor_tensor(hf[:, j % 2, :], hw[:, j % 2, :], Xp[:, bank, QT:2 * QT], ALU.mult)\
                      .then_inc(f_h, 1)

            def reduce_piece(t, k):
                p, i, r, k0, w, diag = piece(k)
                for half in range(2):
                    n = 2 * k + half
                    dve.wait_ge(m_full, 2 * NM * t + n + 1)
                    h = 2 * p + half
                    dst = m0[:, h, i:i + 1] if r == 0 else m1[:, h, i - 4:i - 3]
                    nc.vector.tensor_reduce(dst, Mp[:, n % MB, 0:w], AX.X, ALU.max, negate=True).then_inc(m_red, 1)

            def join_maxima(t, c):
                dve.wait_ge(m_red, after(m_red, 2 * NM * t + (2 * NM if c else 16)))
                q = slice(4 * c, 4 * c + 4)
                if c:
                    nc.vector.tensor_tensor(m0[:, :, q], m0[:, :, q], m1[:], ALU.min).then_inc(m_all, 1)
                    dve.wait_ge(m_all, t + 1)
                dve.wait_ge(m_T, after(m_T, 2 * t + c - 1))
                nc.vector.tensor_copy(mcat[:, c, :, 0, :], m0[:, :, q]).then_inc(m_hi, 1)
                dve.wait_ge(m_hi, 2 * t + c + 1)
                minus_hi(mcat[:, c, :, 1, :], m0[:, :, q], mcat[:, c, :, 0, :]).then_inc(m_cat, 1)

            def body(t, par, second, maxima, front, wo_stage, ffn_stage):
                numbers = uses_of(second, maxima, front, wo_stage, ffn_stage)
                c, f = t - 4, t - 5
                for s in range(NS):
                    m = list(range(M_FROM[s], M_FROM[s] + M_AT[s])) if maxima else []
                    for place in range(2):
                        if front and (s, place) == (1, 0) and not (isinstance(t, int) and t == -1):
                            front_stats(t + 5)
                        if len(m) > place:
                            reduce_piece(t + 1, m[place])
                        if second and (s, place) == (0, 0):
                            join_maxima(t, 1)
                        if maxima and (s, place) == (4, 0):
                            join_maxima(t + 1, 0)
                        if wo_stage and (s, place) == (2, 0):
                            reciprocals(c)
                        if wo_stage and (s, place) == (4, 0):
                            normalise_o(c)
                        if wo_stage and (s, place) == (6, 1):
                            shift(1, c_rs, 2 * c + 1, c_nmr)
                        if ffn_stage and (s, place) == (11, 1):
                            shift(3, f_rs, f + 1, f_nmr)
                        u = X_READ.get((s, 0) if place else (s - 1, 1))
                        if u in numbers:
                            x_reader(*u, numbers[u] % 2, t + 5, t + 1, c, f)
                        if front and (s, place) == (1, 1) and not (isinstance(t, int) and t == -1):
                            front_ln(t + 5)
                        if wo_stage and (s, place) == (5, 1):
                            dve.wait_ge(c_raw, after(c_raw, c + 1))
                            stats(1, an, 2 * c, c_st, c_mv, c_ve)
                        if wo_stage and (s, place) == (8, 0):
                            dve.wait_ge(c_x1, after(c_x1, c + 1))
                            stats(2, x1[par], 2 * c + 1, c_st, c_mv, c_ve)
                        if wo_stage and (s, place) == (9, 0):
                            dve.wait_ge(c_rs, 2 * c + 2)
                            dve.wait_ge(c_T, after(c_T, c))
                            apply_ln(2, xn2, x1[par], c_xn2)
                        if ffn_stage and (s, place) == (10, 1):
                            dve.wait_ge(f_raw, after(f_raw, f + 1))
                            stats(3, yr, f, f_st, f_mv, f_ve)
                    if len(m) > 2:
                        reduce_piece(t + 1, m[2])

            nc.vector.memset(mhalf[:], -0.5)
            nc.vector.memset(ones[:].bitcast(F32), 1.0)
            for i in range(2):
                nc.vector.memset(Ks[i][32:64, :, :].bitcast(F32), 1.0)
                nc.vector.memset(Ks[i][96:128, :, :].bitcast(F32), 1.0)
                nc.vector.memset(Vg[i][:, :, :, DH:32], 1.0)
            nc.vector.memset(spare[:], 0.0).then_inc(small_set, 1)
            front_stats(0)
            front_ln(0)
            dve.wait_ge(proj_in, 48)
            for n, (dst, src, hi) in enumerate(((wqk[1][:, :, 0:D], raw_q, wqk[0][:, :, 0:D]),
                                                (wqk[1][:, :, D:2 * D], raw_k, wqk[0][:, :, D:2 * D]),
                                                (wv[1][:], raw_v, wv[0][:]),
                                                (bo_r[1][:], bo_row[:], bo_r[0][:]))):
                dve.wait_ge(hi_set, n + 1)
                minus_hi(dst, src, hi).then_inc(lo_set, 1)
            nc.vector.tensor_copy(identB[:], identF[:]).then_inc(bf_set, 1)
            nc.vector.tensor_scalar(maskB[:], upF[:], NEG, None, ALU.mult).then_inc(bf_set, 1)
            with dve.Fori(0, 4) as a:
                x_reader("lnT", 0, 0, a, None, None, None)
                front_stats(a + 1)
                x_reader("qk", 0, 1, a, None, None, None)
                front_ln(a + 1)
                x_reader("qk", 1, 0, a, None, None, None)
            each_body(dve, body)

        @blk.gpsimd
        def _(pool):
            def rstd(n, s_ve, s_rs, k):
                pool.wait_ge(s_ve, k + 1)
                nc.gpsimd.tensor_tensor(rs[:, n, :], ve[:, n, :], mhalf[:], ALU.pow).then_inc(s_rs, 1)

            def place_v(t, par, quarters):
                pool.wait_ge(a_vout, after(a_vout, quarters))
                if not (isinstance(t, int) and t < 2):
                    pool.wait_ge(pv_done, after(pv_done, NS * (t - 1)))
                src = v_all[:, bass.ds(8 * ((t // 4) % 2), 8), bass.ds(64 * (t % 4), 64)]\
                    .rearrange("p k (h d) -> p k h d", h=HG)
                nc.gpsimd.tensor_copy(Vg[par][:, :, :, 0:DH], src).then_inc(vg_set, 1)

            def mask(t, s):
                pool.wait_ge(exp_done, after(exp_done, 2 * NS * t + 2 * s + 2))
                nc.gpsimd.tensor_tensor(spare_p[0:1, s + 1:s + 2], spare_p[0:1, 0:1], spare_p[0:1, 0:1],
                                        ALU.add)
                v = Pt[:, s % 2, :, 0:P]
                nc.gpsimd.affine_select(out=v, in_=v, compare_op=ALU.is_ge, fill=0.0, base=0,
                                        pattern=[[0, HG], [1, P]], channel_multiplier=-1).then_inc(p_masked, 1)

            def hidden_lo(f, j):
                pool.wait_ge(f_hi, 8 * f + j + 1)
                if j == 0:
                    pool.wait_ge(f_down, after(f_down, f))
                nc.gpsimd.tensor_tensor(hh[1][:, j, :], hf[:, j % 2, :], hh[0][:, j, :].bitcast(F32), ALU.subtract)\
                  .then_inc(f_lo, 1)

            def body(t, par, second, maxima, front, wo_stage, ffn_stage):
                c, f = t - 4, t - 5
                for s in range(NS):
                    if front and s == 1 and not (isinstance(t, int) and t == -1):
                        rstd(0, a_ve, a_rs, t + 5)
                    if wo_stage and s == 7:
                        pool.wait_ge(c_an, c + 1)
                        pool.wait_ge(xc_in, 16 * (c + 1))
                        nc.gpsimd.tensor_tensor(x1[par], an, xc, ALU.add).then_inc(c_x1, 1)
                    if ffn_stage:
                        for j in LO_BEFORE.get(s, ()):
                            hidden_lo(f, j)
                    if wo_stage and s == 6:
                        rstd(1, c_ve, c_rs, 2 * c)
                    if second and diagonal(s):
                        mask(t, s)
                    if wo_stage and s == 8:
                        rstd(2, c_ve, c_rs, 2 * c + 1)
                    if ffn_stage and s == 10:
                        rstd(3, f_ve, f_rs, f)
                    if ffn_stage:
                        for j in LO_AFTER.get(s, ()):
                            hidden_lo(f, j)
                    if isinstance(t, int) and t == -1 and s == 9:
                        pool.wait_ge(w2_hi, 1)
                        nc.gpsimd.tensor_tensor(w2[1][:], had_b, w2[0][:].bitcast(F32), ALU.subtract)\
                          .then_inc(w2_set, 1)
                    if second and front and not wo_stage and s == 9:
                        pool.wait_ge(w13_hi, t + 1)
                        nc.gpsimd.tensor_tensor(w13_part(1, t), flat[:, bass.ds(1024 * t, 1024)],
                                                w13_part(0, t).bitcast(F32), ALU.subtract).then_inc(w13_set, 1)
                    if maxima and s == 4:
                        place_v(t + 1, (par + 1) % 2, 4 if isinstance(t, int) and t == -1 else t + 5 if front else NQ)
                    if ffn_stage and s == 11:
                        pool.wait_ge(f_yn, f + 1)
                        pool.wait_ge(y_out, after(y_out, 16 * f))
                        nc.gpsimd.tensor_tensor(yo, yr, x1[(par + 1) % 2], ALU.add).then_inc(f_y, 1)

            nc.gpsimd.memset(spare_p[:], 0.0).then_inc(spare_set, 1)
            pool.wait_ge(spare_set, 1)
            pool.wait_ge(small_set, 1)
            with pool.Fori(0, 5) as a:
                rstd(0, a_ve, a_rs, a)

            pool.wait_ge(had_out, 2)
            for n, (src, dst) in enumerate(((had_a, had_b), (had_b, had_a), (had_a, had_b))):
                if n:
                    pool.wait_ge(fly, 4 * n)
                for q in range(4):
                    c = (q >> n << (n + 1)) + q % 2 ** n
                    o = c + 2 ** n
                    nc.gpsimd.tensor_tensor(dst[:, c, :], src[:, c, :], src[:, o, :], ALU.add)
                    nc.gpsimd.tensor_tensor(dst[:, o, :], src[:, c, :], src[:, o, :], ALU.subtract).then_inc(fly, 1)
            each_body(pool, body)


def kernel(**inputs):
    import numpy as np
    import concourse.bacc as bacc
    from concourse.bass_utils import run_bass_kernel_spmd

    n = np.arange(P)
    had = np.ones((1, 1), np.float32)
    while had.shape[0] < P:
        had = np.block([[had, had], [had, -had]])
    arrays = {
        "x": inputs["L0_attn_x"],
        "wqT": inputs["L0_attn_Wq"].T, "wkT": inputs["L0_attn_Wk"].T, "wvT": inputs["L0_attn_Wv"].T,
        "woT": inputs["L0_attn_Wo"].T, "bo": inputs["L0_attn_bo"],
        "w1T": inputs["L0_ffn_W1"].T, "w3T": inputs["L0_ffn_W3"].T, "w2T": inputs["L0_ffn_W2"].T,
        "had": had.astype(np.float32), "ident": np.eye(P, dtype=np.float32),
        "upper": (n[None, :] > n[:, None]).astype(np.float32),
    }
    nc = bacc.Bacc("TRN2", target_bir_lowering=False, num_devices=1)
    feeds, args = {}, []
    for name, a in arrays.items():
        a = np.ascontiguousarray(a)
        feeds[f"in_{name}"] = a
        args.append(nc.dram_tensor(f"in_{name}", a.shape, mybir.dt.from_np(a.dtype), kind="ExternalInput").ap())
    out = nc.dram_tensor("out_0", (B, S, D), F32, kind="ExternalOutput").ap()
    block(nc, *args, out)
    r = run_bass_kernel_spmd(nc, [feeds], core_ids=[0])
    return r.results[0]["out_0"]
```

```python
from contextlib import ExitStack

import concourse.bass as bass
from concourse import mybir

F32 = mybir.dt.float32
F32R = mybir.dt.float32r
BF16 = mybir.dt.bfloat16
ALU = mybir.AluOpType
ACT = mybir.ActivationFunctionType
AX = mybir.AxisListType

P = 128
B, S, D, H = 4, 1024, 256, 1024
HEADS, DH = 16, 16
HG = 4
KC = D // P
QT = 256
NQ = B * S // QT
NT = B * HEADS // HG
NF = H // P
EPS = 1e-5
SCALE = 0.25
NEG = -1e30
CH = 512
LEAD = 16
MB = 3

STEPS = [(c, kb) for c in range(S // CH) for kb in range(4 * c + 4)]
PIECES = [(p, i, r) for c in range(2) for p in range(2) for i in range(4 * c, 4 * c + 4) for r in range(c + 1)]
NS, NM = len(STEPS), len(PIECES)
M_AT = [0, 3, 3, 2, 2, 2, 2, 2, 3, 2, 2, 1]
M_FROM = [sum(M_AT[:s]) for s in range(NS)]


class Plan:

    def __init__(self, uses, halves, places, lo_before, lo_after):
        self.uses = uses
        self.halves = halves
        self.read = {halves.get(u, at): u for at, u in uses.items()}
        self.hi = {u[1]: 2 * at[0] + at[1] + 2 for at, u in uses.items() if u[0] == "ffn"}
        self.lo_before, self.lo_after = lo_before, lo_after
        self.places = places


FULL = Plan(
    {(0, 0): ("ffn", 0), (0, 1): ("ffn", 1), (1, 0): ("maxT", 1), (1, 1): ("ffn", 2), (2, 0): ("ffn", 3),
     (2, 1): ("lnT", 0), (3, 0): ("ffn", 4), (3, 1): ("qk", 0), (4, 0): ("ffn", 5), (4, 1): ("qk", 1),
     (5, 0): ("attn", 0), (5, 1): ("maxT", 0), (6, 0): ("ffn", 6), (7, 0): ("ffn", 7),
     (8, 0): ("down", 0), (10, 0): ("ln2T", 0), (11, 0): ("v", 0)},
    {("down", 0): (9, 1), ("v", 0): (11, 1)},
    {"reciprocals": (2, 0), "normalise_o": (3, 1), "oc_hi": (4, 0), "oc_lo": (4, 1), "stats_an": (5, 1), "rstd_an": 6, "shift_an": (6, 1),
     "an": (7, 0), "x1": 7, "stats_x1": (8, 0), "rstd_x1": 8, "xn2": (9, 0)},
    {1: (0,), 5: (4,), 6: (5,), 7: (6,), 8: (7,)}, {1: (1,), 2: (2,), 3: (3,)})
LATE = Plan(
    {(0, 0): ("ffn", 0), (0, 1): ("ffn", 1), (1, 0): ("maxT", 1), (1, 1): ("ffn", 2), (2, 1): ("ffn", 3),
     (3, 1): ("ffn", 4), (4, 1): ("ffn", 5), (5, 0): ("attn", 0), (5, 1): ("maxT", 0), (6, 0): ("ffn", 6),
     (7, 0): ("ffn", 7), (8, 0): ("down", 0), (10, 0): ("ln2T", 0)},
    {("down", 0): (9, 1)}, FULL.places, FULL.lo_before, FULL.lo_after)
EARLY = Plan(
    {(1, 0): ("maxT", 1), (2, 1): ("lnT", 0), (3, 1): ("qk", 0), (4, 0): ("qk", 1), (4, 1): ("v", 0),
     (5, 1): ("maxT", 0)}, {}, {}, {}, {})
TAIL = Plan(
    {(0, 0): ("ffn", 0), (0, 1): ("ffn", 1), (1, 0): ("ffn", 2), (1, 1): ("ffn", 3), (2, 0): ("ffn", 4),
     (2, 1): ("attn", 0), (3, 0): ("ffn", 5), (3, 1): ("ffn", 6), (4, 0): ("ffn", 7), (8, 0): ("down", 0),
     (10, 0): ("ln2T", 0)},
    {},
    {"reciprocals": (8, 0), "normalise_o": (1, 1), "oc_hi": (1, 1), "oc_lo": (2, 0), "stats_an": (4, 0), "rstd_an": 5, "shift_an": (5, 0),
     "an": (5, 0), "x1": None, "stats_x1": (5, 1), "rstd_x1": 7, "xn2": (6, 0)},
    {1: (0, 1), 2: (2,), 3: (3, 4), 4: (5,), 5: (6,), 6: (7,)}, {})
FRONT_USES = [("lnT", 0), ("v", 0), ("qk", 0), ("qk", 1)]


def plan_of(second, maxima, front, wo_stage):
    if not (second or maxima):
        return TAIL
    return EARLY if not wo_stage else FULL if front else LATE


def uses_of(second, maxima, front, wo_stage, ffn_stage):
    has = {("maxT", 1): second, ("maxT", 0): maxima, "lnT": front, "qk": front, "v": front, "attn": wo_stage, "ln2T": wo_stage,
           "ffn": ffn_stage, "down": ffn_stage}
    uses = plan_of(second, maxima, front, wo_stage or ffn_stage).uses
    order = [uses[k] for k in sorted(uses)]
    return {u: n for n, u in enumerate(u for u in order if has.get(u, has.get(u[0])))}


def ring(maxima):
    return 2 if maxima else 2 + MB


def diagonal(s):
    c, kb = STEPS[s]
    return kb >= 4 * c


def span(s):
    c, kb = STEPS[s]
    q0 = max(CH * c, P * kb)
    return q0, CH * (c + 1) - q0


def piece(k):
    p, i, r = PIECES[k]
    k0 = 512 * r
    w = min(512, P * (i + 1) - k0)
    return p, i, r, k0, w, k0 + w == P * (i + 1)


def each_body(eng, body):
    body(-1, 1, False, True, True, False, False)
    with eng.Fori(0, 2) as i:
        for par in range(2):
            body(2 * i + par, par, True, True, True, False, False)
    body(4, 0, True, True, True, True, False)
    with eng.Fori(2, 5) as i:
        for par in (1, 2):
            body(2 * i + par, par % 2, True, True, True, True, True)
    with eng.Fori(5, 7) as i:
        for par in (1, 2):
            body(2 * i + par, par % 2, True, True, False, True, True)
    body(15, 1, True, False, False, True, True)
    with eng.Fori(8, 10) as i:
        for par in range(2):
            body(2 * i + par, par, False, False, False, True, True)
    body(20, 0, False, False, False, False, True)


def block(nc, x, wqT, wkT, wvT, woT, bo, w1T, w3T, w2T, had, ident, upper, out):
    ctx = ExitStack()
    with ctx:
        def sb(name, shape, dt=F32):
            return ctx.enter_context(nc.sbuf_tensor(name, shape, dt))

        def sem(name):
            return ctx.enter_context(nc.semaphore(name))

        qk_dram = nc.dram_tensor("qk_scratch", [B, 4, 3, P, S], F32).ap()
        o_dram = nc.dram_tensor("o_scratch", [B, 2, HEADS, 32, CH], F32).ap()
        r_dram = nc.dram_tensor("r_scratch", [NQ, HEADS, QT], F32).ap()

        identF = sb("identF", [P, P])
        identB = sb("identB", [P, P], BF16)
        maskB = sb("maskB", [P, P], BF16)
        mhalf = sb("mhalf", [P, 2])
        spare = sb("spare", [P, 2])
        spare_p = sb("spare_p", [P, NS + 1])
        wqk = [sb(f"wqk_{n}", [P, KC, 2 * D], F32R) for n in ("hi", "lo")]
        wv = [sb(f"wv_{n}", [P, KC, D], F32R) for n in ("hi", "lo")]
        wo = [sb(f"wo_{n}", [P, KC, D], F32R) for n in ("hi", "lo")]
        bo_r = [sb(f"bo_{n}", [1, D], F32R) for n in ("hi", "lo")]
        ones = sb("ones", [1, P], F32R)
        w13 = [sb(f"w13_{n}", [P, 2, KC, H], F32R) for n in ("hi", "lo")]
        w2 = [sb(f"w2_{n}", [P, NF, D], F32R) for n in ("hi", "lo")]
        xa = sb("xa", [P, 2, D])
        xn = sb("xn", [P, 2, D])
        xT = [sb(f"xT_{n}", [P, KC, QT], F32R) for n in ("hi", "lo")]
        qk = [sb(f"qk_{n}", [P, 4, QT], F32R) for n in ("hi", "lo")]
        v_all = sb("v_all", [P, 2 * S // P, D])
        Qs = [sb(f"Qs{i}", [P, 2, S], F32R) for i in range(2)]
        Ks = [sb(f"Ks{i}", [P, 2, S], F32R) for i in range(2)]
        Vg = [sb(f"Vg{i}", [P, S // P, HG, 32]) for i in range(2)]
        Pt = sb("Pt", [P, 2, HG, CH])
        m0 = sb("m0", [P, HG, 8])
        m1 = sb("m1", [P, HG, 4])
        mcat = sb("mcat", [P, 2, HG, 2, 4], F32R)
        mrow = sb("mrow", [32, 2, P], F32R)
        On = sb("On", [P, 2, CH])
        work = sb("work", [P, 8, 512])
        xc, oc, an, xn2, yr, yo, th, hf = (work[:, i, :].rearrange("p (j d) -> p j d", j=2) for i in range(8))
        x1 = [sb(f"x1_{i}", [P, 2, D])[:] for i in range(2)]
        oT = [sb(f"oT_{n}", [P, KC, QT], F32R) for n in ("hi", "lo")]
        rb = oT[0][:].bitcast(F32)
        dn = sb("dn", [P, 32])
        dr = sb("dr", [P, 32])
        hw = sb("hw", [P, 2, QT])
        nT = [sb(f"nT_{n}", [P, KC, QT], F32R) for n in ("hi", "lo")]
        hh = [sb(f"hh_{n}", [P, NF, QT], F32R) for n in ("hi", "lo")]
        st6 = sb("st6", [P, 4, 2, 6])
        mv = sb("mv", [P, 4, 2, 2])
        ve = sb("ve", [P, 4, 2])
        rs = sb("rs", [P, 4, 2])
        nmr = sb("nmr", [P, 4, 2])
        raw = Pt[:].rearrange("p a h q -> p (a h q)")
        flat = work[:].rearrange("p a q -> p (a q)")
        raw_q, raw_k, raw_v = (raw[:, i * 512:(i + 1) * 512].rearrange("p (k n) -> p k n", k=KC) for i in range(3))
        hadF, upF, bo_row = On[:, 0, 0:P], On[:, 0, P:2 * P], On[0:1, 1, 0:D]
        raw_wo = raw[:, 1536:2048].rearrange("p (k n) -> p k n", k=KC)
        raw_w2 = raw[:, 2048:4096].rearrange("p (c n) -> p c n", c=NF)
        had_a = flat[:, 0:2048].rearrange("p (c n) -> p c n", c=NF)
        had_b = flat[:, 2048:4096].rearrange("p (c n) -> p c n", c=NF)
        x_early = flat[:, 1536:4096].rearrange("p (q j d) -> p q j d", q=5, j=2)
        raw_w13 = flat.rearrange("p (m k n) -> p m k n", m=2, k=KC)

        def w13_part(half, t):
            return w13[half][:].rearrange("p m k n -> p (m k n)")[:, bass.ds(1024 * t, 1024)]

        Sp = ctx.enter_context(nc.psum_tensor("Sp", [P, 2, 512], F32))
        Vp = ctx.enter_context(nc.psum_tensor("Vp", [P, 512], F32))
        XMp = ctx.enter_context(nc.psum_tensor("XMp", [P, 2 + MB, 512], F32))
        Xp, Mp = XMp, XMp[:, 2:2 + MB, :]

        def X2(bank):
            return Xp[:, bank, :].rearrange("p (j d) -> p j d", j=2)

        consts_in = sem("consts_in")
        proj_in = sem("proj_in")
        w2_in = sem("w2_in")
        w13_in = sem("w13_in")
        small_set = sem("small_set")
        spare_set = sem("spare_set")
        bf_set = sem("bf_set")
        hi_set = sem("hi_set")
        lo_set = sem("lo_set")
        had_done = sem("had_done")
        had_out = sem("had_out")
        fly = sem("fly")
        w2_hi = sem("w2_hi")
        w2_set = sem("w2_set")
        w13_hi = sem("w13_hi")
        w13_set = sem("w13_set")
        x_first, x_rest = sem("x_first"), sem("x_rest")
        xa_in = sem("xa_in")
        a_st, a_mv, a_ve, a_rs, a_xn = (sem(n) for n in ("a_st", "a_mv", "a_ve", "a_rs", "a_xn"))
        a_T, a_hi, a_lo = sem("a_T"), sem("a_hi"), sem("a_lo")
        a_qk, a_qkhi, a_qklo = sem("a_qk"), sem("a_qkhi"), sem("a_qklo")
        qk_out = sem("qk_out")
        a_v, a_vout = sem("a_v"), sem("a_vout")
        stacked = [sem(f"stacked{p}") for p in range(2)]
        vg_set = sem("vg_set")
        m_full, m_red = sem("m_full"), sem("m_red")
        m_all, m_hi, m_cat, m_T, m_row = (sem(n) for n in ("m_all", "m_hi", "m_cat", "m_T", "m_row"))
        mrow_in = [sem(f"mrow_in{c}") for c in range(2)]
        s_full, exp_done = sem("s_full"), sem("exp_done")
        p_masked = sem("p_masked")
        pv_done = sem("pv_done")
        o_copy = sem("o_copy")
        o_out = [sem(f"o_out{c}") for c in range(2)]
        dn_in, rd_out, rb_in, xc_in, oc_in = (sem(n) for n in ("dn_in", "rd_out", "rb_in", "xc_in", "oc_in"))
        c_dr, c_on, c_ohi, c_olo, c_attn, c_raw, c_an, c_x1, c_xn2 = (
            sem(n) for n in ("c_dr", "c_on", "c_ohi", "c_olo", "c_attn", "c_raw", "c_an", "c_x1", "c_xn2"))
        c_st, c_mv, c_ve, c_rs = (sem(n) for n in ("c_st", "c_mv", "c_ve", "c_rs"))
        c_nmr, c_T, c_hi, c_lo = (sem(n) for n in ("c_nmr", "c_T", "c_hi", "c_lo"))
        f_gu, f_th, f_w, f_h, f_hi, f_lo = (sem(n) for n in ("f_gu", "f_th", "f_w", "f_h", "f_hi", "f_lo"))
        f_down, f_raw, f_st, f_mv, f_ve, f_rs, f_nmr, f_yn, f_y, y_out = (
            sem(n) for n in ("f_down", "f_raw", "f_st", "f_mv", "f_ve", "f_rs", "f_nmr", "f_yn", "f_y", "y_out"))
        led = (a_qk, a_qkhi, a_qklo, s_full, exp_done, pv_done, m_red, a_xn, a_v, a_vout, a_T, qk_out, vg_set, m_row, m_T, *mrow_in, o_copy,
               *o_out, rb_in, c_dr, c_on, c_attn, c_raw, c_x1, c_T, c_lo, f_gu, f_lo, f_down, f_raw, f_y, y_out)

        def after(s, n):
            return n + LEAD if any(s is l for l in led) else n

        x_rows = x.rearrange("b (q j p) d -> (b q) p j d", j=2, p=P)
        out_rows = out.rearrange("b (q j p) d -> (b q) p j d", j=2, p=P)

        blk = ctx.enter_context(nc.Block())

        @blk.sync
        def _(sp):
            def load_xa(a):
                sp.wait_ge(a_xn, after(a_xn, a))
                sp.dma_start(xa[:], x_rows[a % NQ]).then_inc(xa_in, 16)

            def store_qk(a):
                sp.wait_ge(a_qkhi, after(a_qkhi, 2 * a + 2))
                sp.wait_ge(a_qklo, after(a_qklo, 2 * a + 2))
                cols = bass.ds((a % 4) * QT, QT)
                for half, m0_, m1_, slot in ((0, 0, 4, 0), (1, 0, 2, 1), (0, 0, 2, 2), (0, 2, 4, 1), (1, 2, 4, 2)):
                    sp.dma_start(qk_dram[a // 4, m0_:m1_, slot, :, cols].rearrange("m p t -> p m t"),
                                 qk[half][:, m0_:m1_, :].bitcast(F32)).then_inc(qk_out, 16)

            def stack(t, par, p):
                if isinstance(t, int) and t < 2:
                    sp.wait_ge(small_set, 1)
                elif p == 0:
                    sp.wait_ge(s_full, after(s_full, 2 * NS * (t - 1)))
                g = t % 4
                for dst, kind in ((Qs, 0), (Ks, 2)):
                    for half in range(2):
                        rows = bass.ds((g % 2) * 64 + (2 * p + half) * DH, DH)
                        sp.dma_start(dst[par][64 * half:64 * half + 48, p, :].bitcast(F32),
                                     qk_dram[(t // 4) % B, kind + g // 2, :, rows, :]).then_inc(stacked[p], 16)

            def maxima_rows(t, par, c, front=False):
                sp.wait_ge(m_row, after(m_row, 2 * t + c + 1))
                for h in range(HG):
                    row = 64 * (h % 2) + 48
                    if front and h == HG - 1:
                        sp.wait_ge(qk_out, after(qk_out, 80 * (t + 5)))
                    sp.dma_start(Qs[par][row:row + 2, h // 2, c * CH:(c + 1) * CH].bitcast(F32),
                                 mrow[8 * h:8 * h + 8, c, :].bitcast(F32)).then_inc(mrow_in[c], 16)

            def store_o(t, c):
                sp.wait_ge(o_copy, after(o_copy, 2 * t + c + 1))
                sp.dma_start(o_dram[t // 4, c, bass.ds((t % 4) * HG, HG)].rearrange("h r q -> (h r) q"),
                             On[:, c, :]).then_inc(o_out[c], 16)

            def load_denominators(c, units):
                sp.wait_ge(c_dr, after(c_dr, c))
                for o in o_out:
                    sp.wait_ge(o, after(o, 16 * units))
                q = c % 4
                sp.dma_start(dn[:], o_dram[(c // 4) % B, q // 2, :, DH, bass.ds((q % 2) * QT, QT)]
                             .rearrange("h (a b) -> h a b", b=32)).then_inc(dn_in, 16)

            def load_o(c, par):
                sp.wait_ge(c_attn, after(c_attn, c))
                sp.wait_ge(c_x1, after(c_x1, c))
                sp.dma_start(xc, x_rows[c]).then_inc(xc_in, 16)
                q = c % 4
                for k in range(KC):
                    sp.dma_start(oc[:, k, :], o_dram[c // 4, q // 2, 8 * k:8 * k + 8, 0:DH,
                                                     bass.ds((q % 2) * QT, QT)]).then_inc(oc_in, 16)

            def spread_reciprocals(c):
                sp.wait_ge(c_dr, after(c_dr, c + 1))
                sp.dma_start(r_dram[c].rearrange("h (a b) -> (h a) b", b=32), dr[:]).then_inc(rd_out, 16)
                sp.wait_ge(c_attn, after(c_attn, c))
                sp.wait_ge(rd_out, 16 * (c + 1))
                for k in range(KC):
                    sp.dma_start(rb[:, k, :], r_dram[c, 8 * k:8 * k + 8].rearrange("h (o t) -> h o t", o=1)
                                 .to_broadcast([8, DH, QT])).then_inc(rb_in, 16)

            def store_y(c):
                sp.wait_ge(f_y, after(f_y, c + 1))
                sp.dma_start(out_rows[c], yo).then_inc(y_out, 16)

            def body(t, par, second, maxima, front, wo_stage, ffn_stage):
                if isinstance(t, int) and t == -1:
                    sp.wait_ge(qk_out, after(qk_out, 80 * 4))
                    for p in range(2):
                        stack(0, 0, p)
                if isinstance(t, int) and t == 4:
                    sp.wait_ge(w13_set, 4)
                if wo_stage and second:
                    load_denominators(t - 4, t)
                if second:
                    maxima_rows(t, par, 1)
                if front:
                    load_xa(t + 6)
                if wo_stage and second:
                    load_o(t - 4, par)
                    spread_reciprocals(t - 4)
                if wo_stage and not second:
                    spread_reciprocals(t - 4)
                    load_o(t - 4, par)
                    load_denominators(t - 3, NT)
                if ffn_stage and not second:
                    store_y(t - 6)
                if front:
                    store_qk(t + 5)
                if second:
                    store_o(t, 0)
                if maxima:
                    maxima_rows(t + 1, (par + 1) % 2, 0, front)
                if maxima:
                    stack(t + 2, par, 0)
                if second:
                    store_o(t, 1)
                if maxima:
                    stack(t + 2, par, 1)
                if ffn_stage and maxima:
                    store_y(t - 5)
                if second and not maxima:
                    load_denominators(t - 3, NT)

            for s in led:
                sp.sem_inc(s, LEAD)
            sp.dma_start(x_early[:, 0], x_rows[0]).then_inc(x_first, 16)
            for dst, src in ((raw_q, wqT), (raw_k, wkT), (raw_v, wvT)):
                sp.dma_start(dst, src.rearrange("(k p) n -> p k n", p=P)).then_inc(proj_in, 16)
            for dst, src in ((identF[:], ident), (hadF, had), (upF, upper),
                             (raw_wo, woT.rearrange("(k p) n -> p k n", p=P)),
                             (bo_row, bo.rearrange("(o n) -> o n", o=1))):
                sp.dma_start(dst, src).then_inc(consts_in, 16)
            for a in range(1, 5):
                sp.dma_start(x_early[:, a], x_rows[a]).then_inc(x_rest, 16)
            sp.dma_start(raw_w2, w2T.rearrange("(c p) n -> p c n", p=P)).then_inc(w2_in, 16)
            with sp.Fori(0, 4) as a:
                store_qk(a)

            def bodies(t, *rest):
                body(t, *rest)
                if isinstance(t, int) and t == -1:
                    sp.wait_ge(w2_set, 1)
                    for m, src in enumerate((w1T, w3T)):
                        sp.dma_start(raw_w13[:, m], src.rearrange("(k p) n -> p k n", p=P)).then_inc(w13_in, 16)

            each_body(sp, bodies)
            store_y(NQ - 1)
            sp.wait_ge(y_out, after(y_out, 16 * NQ))
            sp.wait_ge(xa_in, 16 * (NQ - 4))
            for s in stacked:
                sp.wait_ge(s, 64 * (NT + 1))
            sp.wait_ge(qk_out, after(qk_out, 80 * NQ))
            sp.wait_ge(rd_out, 16 * NQ)
            sp.wait_ge(dn_in, 16 * (NQ + 1))
            for o in o_out:
                sp.wait_ge(o, after(o, 16 * NT))

        @blk.tensor
        def _(pe):
            def split_products(dst, left, right, lcols, rcols, k_chunks, stop=True):
                n = 0
                for lh, rh in ((0, 0), (0, 1), (1, 0)):
                    for k in range(k_chunks):
                        mm = nc.tensor.matmul(dst, left[lh][:, k, lcols], right[rh][:, k, rcols],
                                              start=(n == 0), stop=stop and n == 3 * k_chunks - 1)
                        n += 1
                return mm

            def x_read(kind, j, a, t, c, f):
                s, n = {"lnT": lambda: (a_lo, a + 1), "qk": lambda: (a_qklo, 2 * a + j + 1),
                        "v": lambda: (a_vout, a + 1), "maxT": lambda: (m_row, 2 * (t - j) + j + 1),
                        "attn": lambda: (c_raw, c + 1), "ln2T": lambda: (c_lo, c + 1),
                        "ffn": lambda: (f_h, 8 * f + j + 1), "down": lambda: (f_raw, f + 1)}[kind]()
                pe.wait_ge(s, after(s, n))

            def x_part(kind, j, bank, i, a, t, c, f):
                half = Xp[:, bank, i * QT:(i + 1) * QT]
                if kind == "lnT":
                    if i == 0:
                        pe.wait_ge(a_xn, after(a_xn, a + 1))
                    for k in range(2):
                        mm = nc.tensor.transpose(half[:, k * P:(k + 1) * P], xn[:, k, i * P:(i + 1) * P], identF[:])
                    done = a_T
                elif kind == "qk":
                    if i == 0:
                        pe.wait_ge(a_hi, a + 1)
                        pe.wait_ge(a_lo, a + 1)
                    m = 2 * j + i
                    mm = split_products(half, wqk, xT, slice(m * P, (m + 1) * P), slice(0, QT), KC)
                    done = a_qk
                elif kind == "v":
                    if i == 0:
                        pe.wait_ge(a_hi, a + 1)
                        pe.wait_ge(a_lo, a + 1)
                    mm = split_products(half, xT, wv, slice(i * P, (i + 1) * P), slice(0, D), KC)
                    done = a_v
                elif kind == "maxT":
                    if i == 1:
                        return
                    pe.wait_ge(m_cat, 2 * (t - j) + j + 1)
                    nc.tensor.matmul(Xp[0:32, bank, 0:P], mcat[:, j].rearrange("p h n i -> p (h n i)").bitcast(F32),
                                     identF[:], start=True, stop=True).then_inc(m_T, 1)
                    return
                elif kind == "attn":
                    if i == 0:
                        pe.wait_ge(c_ohi, c + 1)
                        pe.wait_ge(c_olo, c + 1)
                    split_products(half, oT, wo, slice(i * P, (i + 1) * P), slice(0, D), KC, stop=False)
                    for n in range(2):
                        mm = nc.tensor.matmul(half, ones[0:1, :], bo_r[n][0:1, :], start=False, stop=(n == 1))
                    done = c_attn
                elif kind == "ln2T":
                    if i == 0:
                        pe.wait_ge(c_xn2, c + 1)
                    for k in range(2):
                        mm = nc.tensor.transpose(half[:, k * P:(k + 1) * P], xn2[:, k, i * P:(i + 1) * P], identF[:])
                    done = c_T
                elif kind == "ffn":
                    if j == 0 and i == 0:
                        pe.wait_ge(c_hi, f + 1)
                        pe.wait_ge(c_lo, after(c_lo, f + 1))
                    mm = split_products(half, [w13[h][:, i] for h in range(2)], nT, slice(j * P, (j + 1) * P),
                                        slice(0, QT), KC)
                    done = f_gu
                elif kind == "down":
                    for k in range(NF):
                        if i == 0:
                            pe.wait_ge(f_lo, after(f_lo, 8 * f + k + 1))
                        for n, (lh, rh) in enumerate(((0, 0), (0, 1), (1, 0))):
                            mm = nc.tensor.matmul(half, hh[lh][:, k, i * P:(i + 1) * P], w2[rh][:, k, :],
                                                  start=(k == 0 and n == 0), stop=(k == NF - 1 and n == 2))
                    done = f_down
                if i == 1:
                    mm.then_inc(done, 1)

            def max_piece(t, par, k):
                p, i, r, k0, w, diag = piece(k)
                if k in (0, 4):
                    pe.wait_ge(stacked[p], 64 * (t + 1))
                for half in range(2):
                    lo, n = 64 * half, 2 * k + half
                    if not (isinstance(t, int) and t == 0 and n < MB):
                        pe.wait_ge(m_red, after(m_red, 2 * NM * t + n - MB + 1))
                    mm = nc.tensor.matmul(Mp[:, n % MB, 0:w], Qs[par][lo:lo + 48, p, i * P:(i + 1) * P],
                                          Ks[par][lo:lo + 48, p, k0:k0 + w], start=True, stop=not diag)
                    if not diag:
                        mm.then_inc(m_full, 1)
                if diag:
                    for half in range(2):
                        nc.tensor.matmul(Mp[:, (2 * k + half) % MB, w - P:w], identB[:], maskB[:],
                                         start=False, stop=True).then_inc(m_full, 1)

            def scores(t, par, s, p):
                c, kb = STEPS[s]
                q0, n = span(s)
                if kb == 0 and p == 0:
                    pe.wait_ge(mrow_in[c], after(mrow_in[c], 64 * (t + 1)))
                pe.wait_ge(exp_done, after(exp_done, 2 * NS * t + 2 * s + p))
                for half in range(2):
                    lo = 64 * half
                    mm = nc.tensor.matmul(Sp[:, half, 0:n], Ks[par][lo:lo + 50, p, kb * P:(kb + 1) * P],
                                          Qs[par][lo:lo + 50, p, q0:q0 + n], start=True, stop=True)
                mm.then_inc(s_full, 1)

            def pv(t, par, s, part, parts=1):
                c, kb = STEPS[s]
                _, n = span(s)
                lo, hi = part * n // parts, (part + 1) * n // parts
                if part == 0:
                    if s == 0:
                        pe.wait_ge(vg_set, after(vg_set, t + 1))
                    if kb == 0:
                        pe.wait_ge(o_copy, after(o_copy, 2 * t + c))
                    if diagonal(s):
                        pe.wait_ge(p_masked, 8 * t + kb + 1)
                    else:
                        pe.wait_ge(exp_done, after(exp_done, 2 * NS * t + 2 * s + 2))
                for h in range(HG):
                    mm = nc.tensor.matmul(Vp[32 * h:32 * h + 32, CH - n + lo:CH - n + hi], Vg[par][:, kb, h, :],
                                          Pt[:, s % 2, h, lo:hi], start=(kb == 0), stop=(kb == 4 * c + 3))
                if part == parts - 1:
                    mm.then_inc(pv_done, 1)

            def first_uses(t, second, maxima, front, wo_stage, ffn_stage):
                if second:
                    pe.wait_ge(m_row, after(m_row, 2 * t + 1))
                pe.wait_ge(a_vout, after(a_vout, t + 5 if front else NQ))
                if not maxima:
                    pe.wait_ge(m_red, after(m_red, 2 * NM * NT))
                if front:
                    pe.wait_ge(a_qklo, after(a_qklo, 2 * (t + 5)))
                if wo_stage or ffn_stage:
                    pe.wait_ge(c_lo, after(c_lo, t - 4))
                if ffn_stage:
                    pe.wait_ge(f_raw, after(f_raw, t - 5))

            def body(t, par, second, maxima, front, wo_stage, ffn_stage):
                numbers, plan = uses_of(second, maxima, front, wo_stage, ffn_stage), plan_of(second, maxima, front, wo_stage)
                order = list(numbers)
                counts = (t + 5, t + 1, t - 4, t - 5)
                first_uses(t, second, maxima, front, wo_stage, ffn_stage)

                def use_half(s, place, i):
                    for at, u in plan.uses.items():
                        if u not in numbers or (s, place) != (plan.halves.get(u, at) if i else at):
                            continue
                        n = numbers[u]
                        if i == 0 and n >= ring(maxima):
                            x_read(*order[n - ring(maxima)], *counts)
                        x_part(*u, n % ring(maxima), i, *counts)

                for s in range(NS):
                    m = list(range(M_FROM[s], M_FROM[s] + M_AT[s])) if maxima else []
                    for place in range(2):
                        if len(m) > place:
                            max_piece(t + 1, (par + 1) % 2, m[place])
                        if second:
                            scores(t, par, s, place)
                        use_half(s, place, 0)
                        if place == 1 and len(m) > 2:
                            max_piece(t + 1, (par + 1) % 2, m[2])
                        use_half(s, place, 1)
                        if second and s:
                            parts = 1 if wo_stage or diagonal(s - 1) or STEPS[s - 1][1] == 0 else 2
                            if parts == 2 or place == 1:
                                pv(t, par, s - 1, place if parts == 2 else 0, parts)
                if second:
                    pv(t, par, NS - 1, 0)

            pe.wait_ge(consts_in, 16 * 5)
            pe.wait_ge(hi_set, 4)
            pe.wait_ge(lo_set, 4)
            pe.wait_ge(small_set, 1)
            with pe.Fori(0, 4) as a:
                for n, u in enumerate(FRONT_USES):
                    if n >= 2:
                        x_read(*FRONT_USES[n - 2], a, None, None, None)
                    else:
                        pe.wait_ge(a_qklo, after(a_qklo, 2 * a - 1 + n))
                    for i in range(2):
                        x_part(*u, n % 2, i, a, None, None, None)
            pe.wait_ge(bf_set, 2)
            pe.wait_ge(w2_in, 16)

            for c in range(NF):
                if c == NF // 2:
                    pe.wait_ge(had_out, 1)
                mm = nc.tensor.matmul(Sp[:, c // 2 % 2, (c % 2) * D:(c % 2 + 1) * D], hadF, raw_w2[:, c, :],
                                      start=True, stop=True)
                if c % 4 == 3:
                    mm.then_inc(had_done, 1)
            pe.wait_ge(had_out, 2)

            def bodies(t, *rest):
                if isinstance(t, int) and t == 4:
                    pe.wait_ge(w2_set, 1)
                    pe.wait_ge(lo_set, 5)
                    pe.wait_ge(w13_set, 4)
                body(t, *rest)

            each_body(pe, bodies)

        @blk.scalar
        def _(act):
            def copy(dst, src, **kw):
                return nc.scalar.activation(dst, src, ACT.Copy, **kw)

            def x_reader(kind, j, bank, a, t, c, f, reused=True, maxima=True):
                whole = Xp[:, bank, :]
                if kind == "lnT":
                    act.wait_ge(a_T, after(a_T, a + 1))
                    act.wait_ge(a_v, after(a_v, a))
                    act.wait_ge(a_qk, after(a_qk, 2 * a))
                    copy(xT[0][:].rearrange("p k t -> p (k t)"), whole).then_inc(a_hi, 1)
                elif kind == "qk":
                    act.wait_ge(a_qk, after(a_qk, 2 * a + j + 1))
                    if j == 0:
                        act.wait_ge(qk_out, after(qk_out, 80 * a))
                    copy(qk[0][:, 2 * j:2 * j + 2, :], X2(bank)).then_inc(a_qkhi, 1)
                elif kind == "v":
                    act.wait_ge(a_v, after(a_v, a + 1))
                    if reused:
                        act.wait_ge(vg_set, after(vg_set, a - 4))
                    copy(v_all[:, bass.ds(2 * (a % 8), 2), :], X2(bank)).then_inc(a_vout, 1)
                elif kind == "maxT":
                    u = t - j
                    act.wait_ge(m_T, after(m_T, 2 * u + j + 1))
                    act.wait_ge(mrow_in[j], after(mrow_in[j], 64 * u))
                    copy(mrow[:, j, :], Xp[0:32, bank, 0:P]).then_inc(m_row, 1)
                elif kind == "attn":
                    act.wait_ge(c_attn, after(c_attn, c + 1))
                    act.wait_ge(c_x1, after(c_x1, c))
                    copy(an, X2(bank)).then_inc(c_raw, 1)
                elif kind == "ln2T":
                    act.wait_ge(c_T, after(c_T, c + 1))
                    act.wait_ge(f_gu, after(f_gu, 8 * c))
                    copy(nT[0][:].rearrange("p k t -> p (k t)"), whole).then_inc(c_hi, 1)
                elif kind == "ffn":
                    act.wait_ge(f_gu, after(f_gu, 8 * f + j + 1))
                    if j >= 2 and not maxima:
                        act.wait_ge(f_w, 8 * f + j - 1)
                    nc.scalar.activation(th[:, j % 2, :], Xp[:, bank, 0:QT], ACT.Tanh, scale=0.5).then_inc(f_th, 1)
                elif kind == "down":
                    act.wait_ge(f_down, after(f_down, f + 1))
                    act.wait_ge(f_y, after(f_y, f))
                    copy(yr, X2(bank)).then_inc(f_raw, 1)

            def hidden_hi(f, j):
                act.wait_ge(f_h, 8 * f + j + 1)
                if j == 0:
                    act.wait_ge(f_down, after(f_down, f))
                copy(hh[0][:, j, :], hf[:, j % 2, :]).then_inc(f_hi, 1)

            def normalise(n, tile, count, s_nmr, done):
                act.wait_ge(s_nmr, count + 1)
                for i in range(2):
                    last = nc.scalar.activation(tile[:, i, :], tile[:, i, :], ACT.Identity, bias=nmr[:, n, i:i + 1],
                                                scale=rs[:, n, i:i + 1])
                last.then_inc(done, 1)

            def exps(t, s, p):
                _, n = span(s)
                act.wait_ge(s_full, after(s_full, 2 * NS * t + 2 * s + p + 1))
                if p == 0:
                    act.wait_ge(pv_done, after(pv_done, NS * t + s - 1))
                nc.scalar.activation(Pt[:, s % 2, 2 * p:2 * p + 2, 0:n], Sp[:, :, 0:n], ACT.Exp,
                                     scale=SCALE).then_inc(exp_done, 1)

            def copy_o(t, c):
                act.wait_ge(pv_done, after(pv_done, NS * t + 4 + 8 * c))
                act.wait_ge(o_out[c], after(o_out[c], 16 * t))
                copy(On[:, c, :], Vp[:, :]).then_inc(o_copy, 1)

            def body(t, par, second, maxima, front, wo_stage, ffn_stage):
                numbers, plan = uses_of(second, maxima, front, wo_stage, ffn_stage), plan_of(second, maxima, front, wo_stage)
                for s in range(NS):
                    for place in range(2):
                        if ffn_stage:
                            for j, at in plan.hi.items():
                                if 2 * s + place == at:
                                    hidden_hi(t - 5, j)
                        if second:
                            exps(t, s, place)
                        if wo_stage and (s, place) == plan.places["oc_hi"]:
                            act.wait_ge(c_on, after(c_on, t - 3))
                            copy(oT[0][:], oc).then_inc(c_ohi, 1)
                        if wo_stage and (s, place) == plan.places["an"]:
                            normalise(1, an, t - 4, c_nmr, c_an)
                        if second and s == 5 and place == 0:
                            copy_o(t, 0)
                        u = plan.read.get((s, place))
                        if u in numbers:
                            x_reader(*u, numbers[u] % ring(maxima), t + 5, t + 1, t - 4, t - 5, maxima=maxima)
                    if isinstance(t, int) and t == -1 and s == 8:
                        act.wait_ge(fly, 12)
                        copy(w2[0][:], had_b).then_inc(w2_hi, 1)
                    if second and front and not wo_stage and s == 8:
                        act.wait_ge(w13_in, 32)
                        copy(w13_part(0, t), flat[:, bass.ds(1024 * t, 1024)]).then_inc(w13_hi, 1)
                if second:
                    copy_o(t, 1)
                if ffn_stage:
                    normalise(3, yr, t - 5, f_nmr, f_yn)

            act.wait_ge(proj_in, 48)
            copy(wqk[0][:, :, 0:D], raw_q).then_inc(hi_set, 1)
            copy(wqk[0][:, :, D:2 * D], raw_k).then_inc(hi_set, 1)
            copy(wv[0][:], raw_v).then_inc(hi_set, 1)
            act.wait_ge(consts_in, 16 * 5)
            copy(bo_r[0][:], bo_row).then_inc(hi_set, 1)
            copy(wo[0][:], raw_wo).then_inc(hi_set, 1)
            with act.Fori(0, 4) as a:
                for n, u in enumerate(FRONT_USES):
                    x_reader(*u, n % 2, a, None, None, None, reused=False)

            for n in range(2):
                act.wait_ge(had_done, n + 1)
                copy(flat[:, n * 1024:(n + 1) * 1024], Sp[:].rearrange("p b n -> p (b n)"),
                     scale=1.0 / 64).then_inc(had_out, 1)
            each_body(act, body)

        @blk.vector
        def _(dve):
            def minus_hi(dst, src, hi):
                return nc.vector.tensor_tensor(dst, src, hi.bitcast(F32), ALU.subtract)

            def stats(n, src, k, s_st, s_mv, s_ve):
                for i in range(2):
                    last = nc.vector.bn_stats(st6[:, n, i, :], src[:, i, :])
                last.then_inc(s_st, 1)
                dve.wait_ge(s_st, k + 1)
                nc.vector.memset(spare[0:1, 0:1], 0.0)
                for i in range(2):
                    last = nc.vector.bn_aggr(mv[:, n, i, :], st6[:, n, i, :])
                last.then_inc(s_mv, 1)
                dve.wait_ge(s_mv, k + 1)
                nc.vector.tensor_scalar(ve[:, n, :], mv[:, n, :, 1], EPS, None, ALU.add).then_inc(s_ve, 1)

            def apply_ln(n, dst, src, done):
                for i in range(2):
                    last = nc.vector.tensor_scalar(dst[:, i, :], src[:, i, :], mv[:, n, i, 0:1], rs[:, n, i:i + 1],
                                                   ALU.subtract, ALU.mult)
                last.then_inc(done, 1)

            def front_stats(a, early=False):
                if not early:
                    dve.wait_ge(xa_in, 16 * (a - 4))
                stats(0, x_early[:, a] if early else xa, a, a_st, a_mv, a_ve)

            def front_ln(a, early=False):
                dve.wait_ge(a_rs, a + 1)
                dve.wait_ge(a_T, after(a_T, a))
                apply_ln(0, xn, x_early[:, a] if early else xa, a_xn)

            def shift(n, s_rs, k, done):
                dve.wait_ge(s_rs, k)
                nc.vector.scalar_tensor_tensor(nmr[:, n, :], mv[:, n, :, 0], -1.0, rs[:, n, :], ALU.mult, ALU.mult)\
                  .then_inc(done, 1)

            def reciprocals(c):
                dve.wait_ge(dn_in, 16 * (c + 1))
                nc.vector.reciprocal(dr[:], dn[:]).then_inc(c_dr, 1)

            def normalise_o(c):
                dve.wait_ge(rb_in, after(rb_in, 32 * (c + 1)))
                dve.wait_ge(oc_in, 32 * (c + 1))
                nc.vector.tensor_tensor(oc, oc, rb, ALU.mult).then_inc(c_on, 1)

            def x_reader(kind, j, bank, a, t, c, f):
                whole = Xp[:, bank, :]
                if kind == "lnT":
                    dve.wait_ge(a_hi, a + 1)
                    minus_hi(xT[1][:].rearrange("p k t -> p (k t)"), whole, xT[0][:].rearrange("p k t -> p (k t)"))\
                        .then_inc(a_lo, 1)
                elif kind == "qk":
                    dve.wait_ge(a_qkhi, after(a_qkhi, 2 * a + j + 1))
                    minus_hi(qk[1][:, 2 * j:2 * j + 2, :], X2(bank), qk[0][:, 2 * j:2 * j + 2, :])\
                        .then_inc(a_qklo, 1)
                elif kind == "ln2T":
                    dve.wait_ge(c_hi, c + 1)
                    minus_hi(nT[1][:].rearrange("p k t -> p (k t)"), whole, nT[0][:].rearrange("p k t -> p (k t)"))\
                        .then_inc(c_lo, 1)
                elif kind == "ffn":
                    dve.wait_ge(f_th, 8 * f + j + 1)
                    dve.wait_ge(f_lo, after(f_lo, 8 * f + j - 1 if j >= 2 else 8 * f))
                    nc.vector.scalar_tensor_tensor(hw[:, j % 2, :], th[:, j % 2, :], 1.0, Xp[:, bank, 0:QT], ALU.add, ALU.mult)\
                      .then_inc(f_w, 1)
                    dve.wait_ge(f_w, 8 * f + j + 1)
                    nc.vector.tensor_tensor(hf[:, j % 2, :], hw[:, j % 2, :], Xp[:, bank, QT:2 * QT], ALU.mult)\
                      .then_inc(f_h, 1)

            def reduce_piece(t, k):
                p, i, r, k0, w, diag = piece(k)
                for half in range(2):
                    n = 2 * k + half
                    dve.wait_ge(m_full, 2 * NM * t + n + 1)
                    h = 2 * p + half
                    dst = m0[:, h, i:i + 1] if r == 0 else m1[:, h, i - 4:i - 3]
                    nc.vector.tensor_reduce(dst, Mp[:, n % MB, 0:w], AX.X, ALU.max, negate=True).then_inc(m_red, 1)

            def join_maxima(t, c):
                dve.wait_ge(m_red, after(m_red, 2 * NM * t + (2 * NM if c else 16)))
                q = slice(4 * c, 4 * c + 4)
                if c:
                    nc.vector.tensor_tensor(m0[:, :, q], m0[:, :, q], m1[:], ALU.min).then_inc(m_all, 1)
                    dve.wait_ge(m_all, t + 1)
                dve.wait_ge(m_T, after(m_T, 2 * t + c - 1))
                nc.vector.tensor_copy(mcat[:, c, :, 0, :], m0[:, :, q]).then_inc(m_hi, 1)
                dve.wait_ge(m_hi, 2 * t + c + 1)
                minus_hi(mcat[:, c, :, 1, :], m0[:, :, q], mcat[:, c, :, 0, :]).then_inc(m_cat, 1)

            def body(t, par, second, maxima, front, wo_stage, ffn_stage):
                numbers, plan = uses_of(second, maxima, front, wo_stage, ffn_stage), plan_of(second, maxima, front, wo_stage)
                c, f = t - 4, t - 5
                for s in range(NS):
                    m = list(range(M_FROM[s], M_FROM[s] + M_AT[s])) if maxima else []
                    for place in range(2):
                        if front and (s, place) == (1, 0) and not (isinstance(t, int) and t == -1):
                            front_stats(t + 5)
                        if len(m) > place:
                            reduce_piece(t + 1, m[place])
                        if second and (s, place) == (0, 0):
                            join_maxima(t, 1)
                        if maxima and (s, place) == (4, 0):
                            join_maxima(t + 1, 0)
                        if wo_stage and (s, place) == plan.places["reciprocals"]:
                            reciprocals(c if second else c + 1)
                        if wo_stage and (s, place) == plan.places["normalise_o"]:
                            normalise_o(c)
                        if wo_stage and (s, place) == plan.places["shift_an"]:
                            shift(1, c_rs, 2 * c + 1, c_nmr)
                        if ffn_stage and (s, place) == (11, 1):
                            shift(3, f_rs, f + 1, f_nmr)
                        if wo_stage and (s, place) == plan.places["oc_lo"]:
                            dve.wait_ge(c_ohi, c + 1)
                            minus_hi(oT[1][:], oc, oT[0][:]).then_inc(c_olo, 1)
                        u = plan.read.get((s, 0) if place else (s - 1, 1))
                        if u in numbers:
                            x_reader(*u, numbers[u] % ring(maxima), t + 5, t + 1, c, f)
                        if front and (s, place) == (1, 1) and not (isinstance(t, int) and t == -1):
                            front_ln(t + 5)
                        if wo_stage and (s, place) == plan.places["stats_an"]:
                            dve.wait_ge(c_raw, after(c_raw, c + 1))
                            stats(1, an, 2 * c, c_st, c_mv, c_ve)
                        if wo_stage and (s, place) == plan.places["stats_x1"]:
                            if plan.places["x1"] is None:
                                dve.wait_ge(c_an, c + 1)
                                dve.wait_ge(xc_in, 16 * (c + 1))
                                nc.vector.tensor_tensor(x1[par], an, xc, ALU.add).then_inc(c_x1, 1)
                            dve.wait_ge(c_x1, after(c_x1, c + 1))
                            stats(2, x1[par], 2 * c + 1, c_st, c_mv, c_ve)
                        if wo_stage and (s, place) == plan.places["xn2"]:
                            dve.wait_ge(c_rs, 2 * c + 2)
                            dve.wait_ge(c_T, after(c_T, c))
                            apply_ln(2, xn2, x1[par], c_xn2)
                        if ffn_stage and (s, place) == (10, 1):
                            dve.wait_ge(f_raw, after(f_raw, f + 1))
                            stats(3, yr, f, f_st, f_mv, f_ve)
                    if len(m) > 2:
                        reduce_piece(t + 1, m[2])
                if second and not maxima:
                    reciprocals(c + 1)

            nc.vector.memset(mhalf[:], -0.5)
            nc.vector.memset(ones[:].bitcast(F32), 1.0)
            for i in range(2):
                nc.vector.memset(Ks[i][32:64, :, :].bitcast(F32), 1.0)
                nc.vector.memset(Ks[i][96:128, :, :].bitcast(F32), 1.0)
                nc.vector.memset(Vg[i][:, :, :, DH:32], 1.0)
            nc.vector.memset(spare[:], 0.0).then_inc(small_set, 1)
            dve.wait_ge(x_first, 16)
            front_stats(0, early=True)
            front_ln(0, early=True)
            dve.wait_ge(proj_in, 48)
            for n, (dst, src, hi) in enumerate(((wqk[1][:, :, 0:D], raw_q, wqk[0][:, :, 0:D]),
                                                (wqk[1][:, :, D:2 * D], raw_k, wqk[0][:, :, D:2 * D]),
                                                (wv[1][:], raw_v, wv[0][:]),
                                                (bo_r[1][:], bo_row, bo_r[0][:]),
                                                (wo[1][:], raw_wo, wo[0][:]))):
                dve.wait_ge(hi_set, n + 1)
                minus_hi(dst, src, hi).then_inc(lo_set, 1)
            nc.vector.tensor_copy(identB[:], identF[:]).then_inc(bf_set, 1)
            nc.vector.tensor_scalar(maskB[:], upF, NEG, None, ALU.mult).then_inc(bf_set, 1)
            dve.wait_ge(x_rest, 64)
            with dve.Fori(0, 4) as a:
                x_reader("lnT", 0, 0, a, None, None, None)
                front_stats(a + 1, early=True)
                x_reader("qk", 0, 0, a, None, None, None)
                front_ln(a + 1, early=True)
                x_reader("qk", 1, 1, a, None, None, None)
            each_body(dve, body)

        @blk.gpsimd
        def _(pool):
            def rstd(n, s_ve, s_rs, k):
                pool.wait_ge(s_ve, k + 1)
                nc.gpsimd.tensor_tensor(rs[:, n, :], ve[:, n, :], mhalf[:], ALU.pow).then_inc(s_rs, 1)

            def place_v(t, par, quarters):
                pool.wait_ge(a_vout, after(a_vout, quarters))
                if not (isinstance(t, int) and t < 2):
                    pool.wait_ge(pv_done, after(pv_done, NS * (t - 1)))
                src = v_all[:, bass.ds(8 * ((t // 4) % 2), 8), bass.ds(64 * (t % 4), 64)]\
                    .rearrange("p k (h d) -> p k h d", h=HG)
                nc.gpsimd.tensor_copy(Vg[par][:, :, :, 0:DH], src).then_inc(vg_set, 1)

            def mask(t, s):
                pool.wait_ge(exp_done, after(exp_done, 2 * NS * t + 2 * s + 2))
                nc.gpsimd.tensor_tensor(spare_p[0:1, s + 1:s + 2], spare_p[0:1, 0:1], spare_p[0:1, 0:1],
                                        ALU.add)
                v = Pt[:, s % 2, :, 0:P]
                nc.gpsimd.affine_select(out=v, in_=v, compare_op=ALU.is_ge, fill=0.0, base=0,
                                        pattern=[[0, HG], [1, P]], channel_multiplier=-1).then_inc(p_masked, 1)

            def hidden_lo(f, j):
                pool.wait_ge(f_hi, 8 * f + j + 1)
                if j == 0:
                    pool.wait_ge(f_down, after(f_down, f))
                nc.gpsimd.tensor_tensor(hh[1][:, j, :], hf[:, j % 2, :], hh[0][:, j, :].bitcast(F32), ALU.subtract)\
                  .then_inc(f_lo, 1)

            def body(t, par, second, maxima, front, wo_stage, ffn_stage):
                plan = plan_of(second, maxima, front, wo_stage)
                c, f = t - 4, t - 5
                for s in range(NS):
                    if front and s == 1 and not (isinstance(t, int) and t == -1):
                        rstd(0, a_ve, a_rs, t + 5)
                    if wo_stage and s == plan.places["x1"]:
                        pool.wait_ge(c_an, c + 1)
                        pool.wait_ge(xc_in, 16 * (c + 1))
                        nc.gpsimd.tensor_tensor(x1[par], an, xc, ALU.add).then_inc(c_x1, 1)
                    if ffn_stage:
                        for j in plan.lo_before.get(s, ()):
                            hidden_lo(f, j)
                    if wo_stage and s == plan.places["rstd_an"]:
                        rstd(1, c_ve, c_rs, 2 * c)
                    if second and diagonal(s):
                        mask(t, s)
                    if wo_stage and s == plan.places["rstd_x1"]:
                        rstd(2, c_ve, c_rs, 2 * c + 1)
                    if ffn_stage and s == 10:
                        rstd(3, f_ve, f_rs, f)
                    if ffn_stage:
                        for j in plan.lo_after.get(s, ()):
                            hidden_lo(f, j)
                    if isinstance(t, int) and t == -1 and s == 9:
                        pool.wait_ge(w2_hi, 1)
                        nc.gpsimd.tensor_tensor(w2[1][:], had_b, w2[0][:].bitcast(F32), ALU.subtract)\
                          .then_inc(w2_set, 1)
                    if second and front and not wo_stage and s == 9:
                        pool.wait_ge(w13_hi, t + 1)
                        nc.gpsimd.tensor_tensor(w13_part(1, t), flat[:, bass.ds(1024 * t, 1024)],
                                                w13_part(0, t).bitcast(F32), ALU.subtract).then_inc(w13_set, 1)
                    if maxima and s == 4:
                        place_v(t + 1, (par + 1) % 2, 4 if isinstance(t, int) and t == -1 else t + 5 if front else NQ)
                    if ffn_stage and s == 11:
                        pool.wait_ge(f_yn, f + 1)
                        pool.wait_ge(y_out, after(y_out, 16 * f))
                        nc.gpsimd.tensor_tensor(yo, yr, x1[(par + 1) % 2], ALU.add).then_inc(f_y, 1)

            nc.gpsimd.memset(spare_p[:], 0.0).then_inc(spare_set, 1)
            pool.wait_ge(spare_set, 1)
            pool.wait_ge(small_set, 1)
            with pool.Fori(0, 5) as a:
                rstd(0, a_ve, a_rs, a)

            pool.wait_ge(had_out, 2)
            pool.wait_ge(a_xn, after(a_xn, 5))
            for n, (src, dst) in enumerate(((had_a, had_b), (had_b, had_a), (had_a, had_b))):
                if n:
                    pool.wait_ge(fly, 4 * n)
                for q in range(4):
                    c = (q >> n << (n + 1)) + q % 2 ** n
                    o = c + 2 ** n
                    nc.gpsimd.tensor_tensor(dst[:, c, :], src[:, c, :], src[:, o, :], ALU.add)
                    nc.gpsimd.tensor_tensor(dst[:, o, :], src[:, c, :], src[:, o, :], ALU.subtract).then_inc(fly, 1)
            each_body(pool, body)


def kernel(**inputs):
    import numpy as np
    import concourse.bacc as bacc
    from concourse.bass_utils import run_bass_kernel_spmd

    n = np.arange(P)
    had = np.ones((1, 1), np.float32)
    while had.shape[0] < P:
        had = np.block([[had, had], [had, -had]])
    arrays = {
        "x": inputs["L0_attn_x"],
        "wqT": inputs["L0_attn_Wq"].T, "wkT": inputs["L0_attn_Wk"].T, "wvT": inputs["L0_attn_Wv"].T,
        "woT": inputs["L0_attn_Wo"].T, "bo": inputs["L0_attn_bo"],
        "w1T": inputs["L0_ffn_W1"].T, "w3T": inputs["L0_ffn_W3"].T, "w2T": inputs["L0_ffn_W2"].T,
        "had": had.astype(np.float32), "ident": np.eye(P, dtype=np.float32),
        "upper": (n[None, :] > n[:, None]).astype(np.float32),
    }
    nc = bacc.Bacc("TRN2", target_bir_lowering=False, num_devices=1)
    feeds, args = {}, []
    for name, a in arrays.items():
        a = np.ascontiguousarray(a)
        feeds[f"in_{name}"] = a
        args.append(nc.dram_tensor(f"in_{name}", a.shape, mybir.dt.from_np(a.dtype), kind="ExternalInput").ap())
    out = nc.dram_tensor("out_0", (B, S, D), F32, kind="ExternalOutput").ap()
    block(nc, *args, out)
    r = run_bass_kernel_spmd(nc, [feeds], core_ids=[0])
    return r.results[0]["out_0"]
```
